# Optimizing a Trainium2 kernel written in Bass

```python
import numpy as np
import jax
import jax.numpy as jnp

def _softmax(x, axis=-1):
    return jax.nn.softmax(x, axis=axis)

def _gelu(x):
    return jax.nn.gelu(x, approximate=True)

def _silu(x):
    return jax.nn.silu(x)

def _sigmoid(x):
    return jax.nn.sigmoid(x)

def _layernorm(x, axis=-1, eps=1e-05):
    m = jnp.mean(x, axis=axis, keepdims=True)
    v = jnp.var(x, axis=axis, keepdims=True)
    return (x - m) / jnp.sqrt(v + eps)

def _scatter_add(tgt, idx, src, axis=0):
    return tgt.at[idx].add(src)

def _segment_sum(src, seg, n):
    return jax.ops.segment_sum(src, seg, n)
kernel_name = 'mk_gnn_preln_d4_gnn_r64_c71d2c'

def setup_inputs(seed: int=0):
    np.random.seed(seed)
    _w = jnp.asarray

    def _rec_inputs():
        import jax
        import jax.numpy as jnp
        _gk = jax.random.key(seed)
        x = -0.0003713 + 1 * jax.random.normal(jax.random.fold_in(_gk, 1), (100000, 128), jnp.float32)
        src = jax.random.randint(jax.random.fold_in(_gk, 2), (50000,), 0, 100000, jnp.int32)
        dst = jax.random.randint(jax.random.fold_in(_gk, 3), (50000,), 0, 100000, jnp.int32)
        _o = jnp.argsort(dst, stable=True)
        src = src[_o]
        dst = dst[_o]
        edge_attr_64 = 0.000167468 + 1.0002 * jax.random.normal(jax.random.fold_in(_gk, 12), (50000, 64), jnp.float32)
        edge_weight = jax.random.uniform(jax.random.fold_in(_gk, 14), (50000,), jnp.float32, 0.0, 0.999998)
        return (x, src, dst, edge_attr_64, edge_weight)
    x, src, dst, edge_attr_64, edge_weight = _rec_inputs()

    def _L0_gnn_setup():
        import jax, jax.numpy as jnp
        import numpy as np
        N_NODES = 100000
        NODE_DIM = 128
        EDGE_DIM = 64
        HIDDEN_DIM = 256
        N_EDGES = 10000
        key = jax.random.key(seed)
        k1, k2, k3, k4, k5, k6, k7 = jax.random.split(key, 7)
        x = jax.random.normal(k1, (N_NODES, NODE_DIM), dtype=jnp.float32)
        edge_index = jax.random.randint(k2, (2, N_EDGES), 0, N_NODES, dtype=jnp.int64)
        edge_attr = jax.random.normal(k3, (N_EDGES, EDGE_DIM), dtype=jnp.float32)
        in_dim = 2 * NODE_DIM + EDGE_DIM
        lim1 = 1.0 / np.sqrt(in_dim)
        lim2 = 1.0 / np.sqrt(HIDDEN_DIM)
        W1 = jax.random.uniform(k4, (in_dim, HIDDEN_DIM), minval=-lim1, maxval=lim1, dtype=jnp.float32)
        b1 = jax.random.uniform(k5, (HIDDEN_DIM,), minval=-lim1, maxval=lim1, dtype=jnp.float32)
        W2 = jax.random.uniform(k6, (HIDDEN_DIM, NODE_DIM), minval=-lim2, maxval=lim2, dtype=jnp.float32)
        b2 = jax.random.uniform(k7, (NODE_DIM,), minval=-lim2, maxval=lim2, dtype=jnp.float32)
        return {'x': x, 'edge_index': edge_index, 'edge_attr': edge_attr, 'W1': W1, 'b1': b1, 'W2': W2, 'b2': b2}
    _L0_gnn_all = _L0_gnn_setup()
    _L0_gnn_in = {k: v for k, v in _L0_gnn_all.items() if k in ('W1', 'b1', 'W2', 'b2')}
    del _L0_gnn_all

    def _L1_gnn_setup():
        import jax, jax.numpy as jnp
        import numpy as np
        N_NODES = 100000
        N_EDGES = 10000
        DIM = 128
        key = jax.random.key(seed)
        k1, k2, k3, k4, k5 = jax.random.split(key, 5)
        x = jax.random.normal(k1, (N_NODES, DIM), dtype=jnp.float32)
        edge_index = jax.random.randint(k2, (2, N_EDGES), 0, N_NODES, dtype=jnp.int64)
        edge_weight = jax.random.uniform(k3, (N_EDGES,), dtype=jnp.float32)
        W = jax.random.normal(k4, (DIM, DIM), dtype=jnp.float32) * (1.0 / np.sqrt(DIM))
        b = jax.random.normal(k5, (DIM,), dtype=jnp.float32) * 0.01
        return {'x': x, 'edge_index': edge_index, 'edge_weight': edge_weight, 'W': W, 'b': b}
    _L1_gnn_all = _L1_gnn_setup()
    _L1_gnn_in = {k: v for k, v in _L1_gnn_all.items() if k in ('W', 'b')}
    del _L1_gnn_all

    def _L2_gnn_setup():
        import jax, jax.numpy as jnp
        import numpy as np
        N = 50000
        E = 12500
        D_IN = 128
        D_HID = 512
        D_OUT = 128
        key = jax.random.key(seed)
        k0, k1, k2, k3 = jax.random.split(key, 4)
        x = jax.random.normal(k0, (N, D_IN), dtype=jnp.float32)
        edge_index = jax.random.randint(k1, (2, E), 0, N, dtype=jnp.int64)
        W1 = jax.random.normal(k2, (D_IN, D_HID), dtype=jnp.float32) / np.float32(np.sqrt(D_IN))
        b1 = jnp.zeros((D_HID,), dtype=jnp.float32)
        W2 = jax.random.normal(k3, (D_HID, D_OUT), dtype=jnp.float32) / np.float32(np.sqrt(D_HID))
        b2 = jnp.zeros((D_OUT,), dtype=jnp.float32)
        return {'x': x, 'edge_index': edge_index, 'W1': W1, 'b1': b1, 'W2': W2, 'b2': b2}
    _L2_gnn_all = _L2_gnn_setup()
    _L2_gnn_in = {k: v for k, v in _L2_gnn_all.items() if k in ('W1', 'b1', 'W2', 'b2')}
    del _L2_gnn_all

    def _L3_gnn_setup():
        import jax, jax.numpy as jnp
        import numpy as np
        N_NODES = 50000
        N_EDGES = 12500
        IN_FEATS = 128
        OUT_FEATS = 128
        key = jax.random.key(seed)
        k1, k2, k3, k4 = jax.random.split(key, 4)
        feature = jax.random.normal(k1, (N_NODES, IN_FEATS), dtype=jnp.float32)
        src = jax.random.randint(k2, (N_EDGES,), 0, N_NODES, dtype=jnp.int32)
        dst = jax.random.randint(k3, (N_EDGES,), 0, N_NODES, dtype=jnp.int32)
        W = jax.random.normal(k4, (IN_FEATS, OUT_FEATS), dtype=jnp.float32) * (1.0 / np.sqrt(IN_FEATS))
        b = jnp.zeros((OUT_FEATS,), dtype=jnp.float32)
        return {'feature': feature, 'src': src, 'dst': dst, 'W': W, 'b': b}
    _L3_gnn_all = _L3_gnn_setup()
    _L3_gnn_in = {k: v for k, v in _L3_gnn_all.items() if k in ('W', 'b')}
    del _L3_gnn_all
    return {'x': x, 'src': src, 'dst': dst, 'edge_attr_64': edge_attr_64, 'edge_weight': edge_weight, 'L0_gnn_W1': _L0_gnn_in['W1'], 'L0_gnn_b1': _L0_gnn_in['b1'], 'L0_gnn_W2': _L0_gnn_in['W2'], 'L0_gnn_b2': _L0_gnn_in['b2'], 'L1_gnn_W': _L1_gnn_in['W'], 'L1_gnn_b': _L1_gnn_in['b'], 'L2_gnn_W1': _L2_gnn_in['W1'], 'L2_gnn_b1': _L2_gnn_in['b1'], 'L2_gnn_W2': _L2_gnn_in['W2'], 'L2_gnn_b2': _L2_gnn_in['b2'], 'L3_gnn_W': _L3_gnn_in['W'], 'L3_gnn_b': _L3_gnn_in['b']}

def reference(x, src, dst, edge_attr_64, edge_weight, L0_gnn_W1, L0_gnn_b1, L0_gnn_W2, L0_gnn_b2, L1_gnn_W, L1_gnn_b, L2_gnn_W1, L2_gnn_b1, L2_gnn_W2, L2_gnn_b2, L3_gnn_W, L3_gnn_b):
    import jax
    import jax.numpy as jnp

    def _L0_gnn_ref(x, edge_index, edge_attr, W1, b1, W2, b2):
        import jax, jax.numpy as jnp
        import numpy as np
        N_NODES = 100000
        NODE_DIM = 128
        EDGE_DIM = 64
        HIDDEN_DIM = 256
        N_EDGES = 10000
        row = edge_index[0]
        col = edge_index[1]
        msg = jnp.concatenate([x[row], x[col], edge_attr], axis=-1)
        h = jax.nn.relu(msg @ W1 + b1)
        msg_out = h @ W2 + b2
        out = jax.ops.segment_sum(msg_out, row, num_segments=x.shape[0])
        return out

    def _L1_gnn_ref(x, edge_index, edge_weight, W, b):
        import jax, jax.numpy as jnp
        import numpy as np
        N_NODES = 100000
        N_EDGES = 10000
        DIM = 128
        row, col = (edge_index[0], edge_index[1])
        msgs = edge_weight[:, None] * x[row]
        agg = jax.ops.segment_sum(msgs, col, num_segments=x.shape[0])
        return agg @ W.T + b

    def _L2_gnn_ref(x, edge_index, W1, b1, W2, b2):
        import jax, jax.numpy as jnp
        import numpy as np
        N = 50000
        E = 12500
        D_IN = 128
        D_HID = 512
        D_OUT = 128
        'AGCN forward (eval mode: dropout is identity).\n            GCNConv: out = D^{-1/2} (A + I) D^{-1/2} X W + b, followed by ReLU.\n            Aggregation is linear, so we commute it with the matmul per layer to\n            keep edge messages in the 128-dim space (same math as PyG GCNConv).\n            '
        n = x.shape[0]
        loop = jnp.arange(n)
        src = jnp.concatenate([edge_index[0], loop])
        dst = jnp.concatenate([edge_index[1], loop])
        deg = jax.ops.segment_sum(jnp.ones(dst.shape, x.dtype), dst, num_segments=n)
        dinv = jnp.where(deg > 0, jax.lax.rsqrt(deg), jnp.zeros_like(deg))
        norm = (dinv[src] * dinv[dst])[:, None]

        def agg(h):
            return jax.ops.segment_sum(h[src] * norm, dst, num_segments=n)
        h = jax.nn.relu(agg(x) @ W1 + b1)
        h = jax.nn.relu(agg(h @ W2) + b2)
        return h

    def _L3_gnn_ref(feature, src, dst, W, b):
        import jax, jax.numpy as jnp
        import numpy as np
        N_NODES = 50000
        N_EDGES = 12500
        IN_FEATS = 128
        OUT_FEATS = 128
        msgs = feature[src]
        agg = jax.ops.segment_sum(msgs, dst, num_segments=feature.shape[0])
        h = jnp.dot(agg, W) + b
        return jax.nn.relu(h)
    edge_index = jnp.stack([src, dst])
    h = jnp.maximum(_layernorm(x, axis=-1), 0.0)
    x = x + _L0_gnn_ref(h, edge_index, edge_attr_64, L0_gnn_W1, L0_gnn_b1, L0_gnn_W2, L0_gnn_b2)
    h = jnp.maximum(_layernorm(x, axis=-1), 0.0)
    x = x + _L1_gnn_ref(h, edge_index, edge_weight, L1_gnn_W, L1_gnn_b)
    h = jnp.maximum(_layernorm(x, axis=-1), 0.0)
    x = x + _L2_gnn_ref(h, edge_index, L2_gnn_W1, L2_gnn_b1, L2_gnn_W2, L2_gnn_b2)
    h = jnp.maximum(_layernorm(x, axis=-1), 0.0)
    x = x + _L3_gnn_ref(h, src, dst, L3_gnn_W, L3_gnn_b)
    return x

_drawn_inputs = setup_inputs


def setup_inputs(seed=0):
    import zlib

    import numpy as np

    out = dict(_drawn_inputs(seed))
    spreads = {'L2_gnn_b1': (0.0, 0.1), 'L2_gnn_b2': (0.0, 0.1), 'L3_gnn_b': (0.0, 0.1)}
    factors = {'L0_gnn_b1': 4.518, 'L1_gnn_b': 5.98}
    for name, (base, spread) in spreads.items():
        noise = np.random.default_rng([zlib.crc32(name.encode()), seed]).standard_normal(out[name].shape)
        drawn = base * np.exp(spread * noise) if base else spread * noise
        out[name] = jnp.asarray(drawn.astype(out[name].dtype))
    for name, factor in factors.items():
        out[name] = (out[name] * factor).astype(out[name].dtype)
    return out
```

```python
import concourse.bass as bass
from concourse import mybir
from contextlib import ExitStack

F32 = mybir.dt.float32
I32 = mybir.dt.int32
ALU = mybir.AluOpType
ACT = mybir.ActivationFunctionType

D = 128
N = 100000
E = 50000
NODE_TURNS = -(-N // 512)
NP = NODE_TURNS * 512
EDGE_TURNS = -(-E // 512)
EP = EDGE_TURNS * 512
DUMMY = N
PAD_INDEX = N + 300
DW = D + 4
EPS = 1e-5
SCATTER_LAG = 3
assert DUMMY + 256 <= PAD_INDEX < NP


class Turn:

    def __init__(self, n, slot, use):
        self.n, self.slot, self.use = n, slot, use

    def before(self):
        if isinstance(self.n, int) and self.n == 0:
            return None
        return Turn(self.n - 1, 1 - self.slot, self.use - 1 + self.slot)


def turns(eng, count, lag, step):

    def fixed(n):
        return Turn(n, n % 2, n // 2) if 0 <= n < count else None

    first = lag + 2
    first += (count - first) % 2
    for c in range(first):
        step(fixed(c), fixed(c - lag))
    with eng.Fori(0, (count - first) // 2) as i:
        for u in range(2):
            c, o = first + u, first + u - lag
            step(Turn(2 * i + c, c % 2, i + c // 2), Turn(2 * i + o, o % 2, i + o // 2))
    for c in range(count, count + lag):
        step(None, fixed(c - lag))


def wait_past(eng, sem, value):
    if not isinstance(value, int) or value > 0:
        eng.wait_ge(sem, value)


class Steps:

    def __init__(self, eng, sem, per_turn):
        self.eng, self.sem, self.per_turn, self.turn, self.done = eng, sem, per_turn, None, 0

    def begin(self, turn):
        self.turn, self.done = turn, 0

    def inc(self, instruction):
        self.done += 1
        instruction.then_inc(self.sem, 1)

    def wait(self):
        self.eng.wait_ge(self.sem, self.turn.n * self.per_turn + self.done)

    def end(self):
        assert self.done == self.per_turn, (self.done, self.per_turn)


def build(nc, x, src, dst, ea, ew, m1_w1, m1_b1, m1_w2, m1_b2, l1_w, l1_b, g_w1, g_b1, g_w2, g_b2, l3_w, l3_b, out):
    ctx = ExitStack()

    def sb(name, shape, dt=F32):
        return ctx.enter_context(nc.sbuf_tensor(name, shape, dt))

    def sem(name):
        return ctx.enter_context(nc.semaphore(name))

    def dram(name, shape, dt=F32):
        return nc.dram_tensor(name, shape, dt, kind="Internal").ap()

    with ctx:
        src_pad = dram("src_pad", [EP])
        dst_pad = dram("dst_pad", [EP])
        x1 = dram("x1", [NP, D])
        d1 = dram("d1", [NP, DW])
        x2 = dram("x2", [NP, D])
        h2 = dram("h2", [NP, D])
        s2 = dram("s2", [NP, D])
        z2 = dram("z2", [NP, D])
        t2 = dram("t2", [NP, D])
        x3 = dram("x3", [NP, D])
        s3 = dram("s3", [NP, D])

        ident = sb("ident", [128, 128])
        before = sb("before", [128, 2, 256])
        dummy_i = sb("dummy_i", [128, 4], I32)
        dummy_f = sb("dummy_f", [128, 4])
        zero = sb("zero", [128, 8 * DW])
        eps_c = sb("eps_c", [128, 1])
        list_i = sb("list_i", [112, 2, EP // 112], I32)
        list_f = sb("list_f", [112, 2, EP // 112])
        w1s, w1d = sb("w1s", [128, 256]), sb("w1d", [128, 256])
        w1e = sb("w1e", [64, 256])
        b1c = sb("b1c", [128, 2])
        w2c = sb("w2c", [128, 2, 128])
        b2r = sb("b2r", [128, 128])
        l1w = sb("l1w", [128, 128])
        l1wT = sb("l1wT", [128, 128])
        l1b = sb("l1b", [128, 128])
        gw1 = sb("gw1", [128, 512])
        gb1 = sb("gb1", [128, 4])
        gw2 = sb("gw2", [128, 4, 128])
        gb2 = sb("gb2", [128, 128])
        l3w = sb("l3w", [128, 128])
        l3b = sb("l3b", [128, 128])
        src_f = sb("src_f", [128, EP // 128 + 4])
        dst_f = sb("dst_f", [128, EP // 128 + 4])
        w_f = sb("w_f", [128, EP // 128])
        leader = sb("leader", [128, EP // 128], I32)
        dinv = sb("dinv", [128, 4 * NODE_TURNS])

        rows = sb("rows", [128, 2, 8, 128])
        xn = sb("xn", [128, 8, 128])
        eav = sb("eav", [128, 2, 4, 64])
        idx_row = sb("idx_row", [128, 2, 512])
        gidx = sb("gidx", [128, 2, 8], I32)
        key = sb("key", [128, 2, 4])
        sidx = sb("sidx", [128, 2, 4], I32)
        eq = sb("eq", [128, 2, 4, 256])
        junk = sb("junk", [128, 4, 256])
        wkey = sb("wkey", [128, 2, 4])
        tmp = sb("tmp", [128, 2, 512])
        stats = sb("stats", [128, 8, 6])
        mv = sb("mv", [128, 2, 8, 2])
        sd = sb("sd", [128, 2, 8])
        rsd = sb("rsd", [128, 2, 8])
        rstd = sb("rstd", [128, 2, 8])
        nmr = sb("nmr", [128, 2, 8])
        cnt = sb("cnt", [128, 4])
        degree = sb("degree", [128, 2, 4])
        off = sb("off", [128, 4])
        off2 = sb("off2", [128, 4])
        hTs, hTd = sb("hTs", [128, 512]), sb("hTd", [128, 512])
        eT = sb("eT", [64, 512])
        hid = sb("hid", [128, 4, 512])
        msg = sb("msg", [128, 4, 128])
        mout = sb("mout", [128, 2, 4, 128])
        dout = sb("dout", [128, 2, 4, DW])
        na = sb("na", [128, 2, 512])
        nb = sb("nb", [128, 2, 4 * DW])
        nt = sb("nt", [128, 2, 512])
        no = sb("no", [128, 2, 512])

        bank = [ctx.enter_context(nc.psum_tensor(f"bank{i}", [128, 512], F32)) for i in range(8)]


        pad_ready = sem("pad_index_set")
        zero_ready = sem("zero_set")
        ready = sem("constants_ready")
        loads = sem("constants_loaded")
        lists_in = sem("lists_in")
        lists_float = sem("lists_float")
        lists_out = sem("lists_out")
        spare_set = sem("spare_group_set")
        w_zeroed = sem("weights_zeroed")
        tables = sem("tables_loaded")
        x1_set = sem("x1_set")
        d1_zeroed = sem("d1_zeroed")
        s3_zeroed = sem("s3_zeroed")
        gates = sem("pool_gates")
        tables_f = sem("tables_float")
        wT_psum = sem("l1_weight_transposed")
        wT_out = sem("l1_weight_copied")

        class Edge:

            def __init__(self, tag):
                self.gidx_ready = sem(f"{tag}_gidx_ready")
                self.gathered = [sem(f"{tag}_gathered{u}") for u in range(2)]
                self.row_loaded = [sem(f"{tag}_idx_row_loaded{u}") for u in range(2)]
                self.row_read = sem(f"{tag}_idx_row_read")
                self.var_ready = sem(f"{tag}_var_ready")
                self.sd_ready = sem(f"{tag}_sd_ready")
                self.norm_ready = sem(f"{tag}_norm_ready")
                self.xn_ready = sem(f"{tag}_xn_ready")
                self.eq_ready = sem(f"{tag}_eq_ready")
                self.sidx_ready = sem(f"{tag}_sidx_ready")
                self.summed = sem(f"{tag}_summed")
                self.out_ready = sem(f"{tag}_out_ready")
                self.scattered = sem(f"{tag}_scattered")
                self.dve = sem(f"{tag}_dve_steps")

        class Node:

            def __init__(self, tag):
                self.loaded = [sem(f"{tag}_loaded{u}") for u in range(2)]
                self.inputs_read = sem(f"{tag}_inputs_read")
                self.turned = sem(f"{tag}_turned")
                self.turned_out = sem(f"{tag}_turned_out")
                self.product = sem(f"{tag}_product")
                self.result = sem(f"{tag}_result")
                self.stored = [sem(f"{tag}_stored{u}") for u in range(2)]
                self.dve = sem(f"{tag}_dve_steps")

        mlp, wag, gc1, gc2, gra = (Edge(t) for t in ("mlp", "wag", "gc1", "gc2", "gra"))
        n_x2, n_gcn, n_x3, n_out = (Node(t) for t in ("n_x2", "n_gcn", "n_x3", "n_out"))
        n_x3.inputs_read, n_out.inputs_read = n_x3.result, n_out.result
        ea_loaded = [sem(f"ea_loaded{u}") for u in range(2)]
        turned = sem("mlp_turned")
        turned_out = sem("mlp_turned_out")
        hid_psum = sem("mlp_hidden")
        hid_out = sem("mlp_hidden_out")
        msg_psum = sem("mlp_messages")
        msg_out = sem("mlp_messages_out")
        aggT_psum = sem("wag_sums_transposed")
        aggT_out = sem("wag_sums_copied")
        x2_ready = sem("x2_ready")
        x2_norm = sem("x2_norm_ready")
        x2_norm_steps = sem("x2_norm_steps")
        sd_ready = sem("x2_sd_ready")
        ghid_psum = sem("gcn_hidden")
        ghid_act = sem("gcn_hidden_act")
        ghid_dve = sem("gcn_hidden_dve")

        ea_flat = ea.rearrange("e f -> (e f)")
        last_rows = N - (NODE_TURNS - 1) * 512
        full = (E // 256) * 256
        rest = (E - full) // 2
        n_const = 14
        HALF_NODES = NODE_TURNS // 2

        def nodes(a, n, count=512):
            return a[bass.ds(n * 512, count), :].rearrange("(p k) f -> p (k f)", k=4)

        def by4(t):
            return t.rearrange("p (s f) -> p s f", s=4)

        def row4(t):
            return t[:, :].rearrange("p (a f) -> p a f", a=1).to_broadcast([128, 4, 128])

        def dinv4(n):
            return dinv[:, bass.ds(n * 4, 4)].rearrange("p (s a) -> p s a", a=1).to_broadcast([128, 4, 128])

        block = ctx.enter_context(nc.Block())

        @block.sync
        def _(sp):
            w = EP // 112
            sp.wait_ge(pad_ready, 1)
            for j, of in enumerate((src, dst)):
                sp.dma_start(list_i[0:E // w, j, :], of[0:E // w * w].rearrange("(a b) -> a b", b=w)).then_inc(lists_in, 16)
                sp.dma_start(list_i[E // w:E // w + 1, j, 0:E % w], of[E // w * w:E].rearrange("(a b) -> a b", a=1)).then_inc(lists_in, 16)
            sp.wait_ge(lists_float, 1)
            for j, to in enumerate((src_pad, dst_pad)):
                sp.dma_start(to.rearrange("(a b) -> a b", b=w), list_f[:, j, :]).then_inc(lists_out, 16)
            sp.wait_ge(lists_out, 32)
            for tab, of in ((src_f, src_pad), (dst_f, dst_pad)):
                sp.wait_ge(spare_set, 2)
                sp.dma_start(tab[:, 0:EP // 128].rearrange("p (c k) -> p c k", k=2),
                             of.rearrange("(c p k) -> p c k", p=128, k=2)).then_inc(tables, 16)
            sp.wait_ge(w_zeroed, 1)
            wv = w_f[:, :].rearrange("p (c k) -> p c k", k=2)
            sp.dma_start(wv[:, 0:full // 256, :], ew[0:full].rearrange("(c p k) -> p c k", p=128, k=2)).then_inc(tables, 16)
            sp.dma_start(wv[0:rest, full // 256, :], ew[full:E].rearrange("(p k) -> p k", k=2)).then_inc(tables, 16)
            consts = [(w1s[:, :], m1_w1[0:128, :]), (w1d[:, :], m1_w1[128:256, :]), (w1e[:, :], m1_w1[256:320, :]),
                      (w2c[:, :, :], m1_w2.rearrange("(c p) n -> p c n", p=128)), (l1w[:, :], l1_w), (gw1[:, :], g_w1),
                      (gw2[:, :, :], g_w2.rearrange("(c p) n -> p c n", p=128)), (l3w[:, :], l3_w)]
            consts += [(to[:, :], of.rearrange("(a n) -> a n", a=1).to_broadcast([128, 128]))
                       for to, of in ((b2r, m1_b2), (l1b, l1_b), (gb2, g_b2), (l3b, l3_b))]
            for to, of in consts:
                sp.dma_start(to, of).then_inc(loads, 16)
            with nc.allow_non_contiguous_dma(reason="bias vectors as columns, once"):
                sp.dma_start(b1c[:, :], m1_b1.rearrange("(c p) -> p c", p=128)).then_inc(loads, 16)
                sp.dma_start(gb1[:, :], g_b1.rearrange("(c p) -> p c", p=128)).then_inc(loads, 16)
            assert len(consts) + 2 == n_const

            def load_idx_row(e, of, t):
                wait_past(sp, e.row_read, t.n - 1)
                sp.dma_start(idx_row[:, t.slot, :], of[bass.ds(t.n * 512, 512)].rearrange("(a n) -> a n", a=1).to_broadcast([128, 512]))\
                    .then_inc(e.row_loaded[t.slot], 16)

            def mlp_loads(new, old):
                load_idx_row(mlp, src_pad, new)
                wait_past(sp, turned, 3 * (new.n - 1))
                to = eav[:, new.slot, :, :].rearrange("p (b k) f -> p b (k f)", k=2)
                if isinstance(new.n, int) and new.n == EDGE_TURNS - 1:
                    flat = ea_flat[new.n * 512 * 64:E * 64]
                    sp.dma_start(to[:, 0, :], flat[0:256 * 64].rearrange("(p j) -> p j", p=128)).then_inc(ea_loaded[new.slot], 16)
                    sp.dma_start(to[0:rest, 1, :], flat[256 * 64:].rearrange("(p j) -> p j", p=rest)).then_inc(ea_loaded[new.slot], 16)
                else:
                    of = ea_flat[bass.ds(new.n * (512 * 64), 512 * 64)]
                    sp.dma_start(to, of.rearrange("(b p j) -> p b j", b=2, p=128)).then_inc(ea_loaded[new.slot], 16)

            turns(sp, EDGE_TURNS - 1, 0, mlp_loads)
            mlp_loads(Turn(EDGE_TURNS - 1, (EDGE_TURNS - 1) % 2, (EDGE_TURNS - 1) // 2), None)

            def node_pass(s, ins, outs):
                def step(new, old):
                    if new:
                        wait_past(sp, s.inputs_read, new.n - 1)
                        for of, buf in ins:
                            sp.dma_start(buf[:, new.slot, 0:4 * of.shape[1]], nodes(of, new.n)).then_inc(s.loaded[new.slot], 16)
                    if old:
                        for to, buf, result in outs:
                            sp.wait_ge(result, old.n + 1)
                            if to is out and isinstance(old.n, int) and old.n == NODE_TURNS - 1:
                                sp.dma_start(nodes(out, old.n, last_rows), buf[0:last_rows // 4, old.slot, :]).then_inc(s.stored[old.slot], 16)
                            else:
                                sp.dma_start(nodes(to, old.n), buf[:, old.slot, :]).then_inc(s.stored[old.slot], 16)
                turns(sp, NODE_TURNS, 2, step)

            def idx_rows(e, before_):
                sp.wait_ge(before_.row_read, EDGE_TURNS)
                turns(sp, EDGE_TURNS, 0, lambda new, old: load_idx_row(e, dst_pad, new))

            idx_rows(wag, mlp)
            sp.wait_ge(wag.scattered, 64 * EDGE_TURNS)
            node_pass(n_x2, [(x1, na), (d1, nb)], [(x2, nt, x2_ready), (h2, no, n_x2.result), (s2, no, n_x2.result)])
            idx_rows(gc1, wag)
            sp.wait_ge(gc1.scattered, 64 * EDGE_TURNS)
            node_pass(n_gcn, [(s2, na)], [(z2, no, n_gcn.result), (t2, no, n_gcn.result)])
            idx_rows(gc2, gc1)
            sp.wait_ge(gc2.scattered, 64 * EDGE_TURNS)
            node_pass(n_x3, [(x2, na), (t2, nb)], [(x3, no, n_x3.result)])
            idx_rows(gra, gc2)
            sp.wait_ge(gra.scattered, 64 * EDGE_TURNS)
            node_pass(n_out, [(x3, na), (s3, nb)], [(out, no, n_out.result)])
            for u in range(2):
                sp.wait_ge(n_out.stored[u], 16 * HALF_NODES)

        @block.gpsimd
        def _(pool):
            nc.gpsimd.memset(list_i[:, :, :], PAD_INDEX).then_inc(pad_ready, 1)
            nc.gpsimd.memset(zero[:, :], 0.0).then_inc(zero_ready, 1)
            nc.gpsimd.memset(eps_c[:, :], EPS).then_inc(zero_ready, 1)
            nc.gpsimd.memset(ident[:, :], 0.0).then_inc(ready, 1)
            nc.gpsimd.memset(before[:, :, :], 1.0).then_inc(ready, 1)
            pool.wait_ge(ready, 2)
            nc.gpsimd.affine_select(out=ident[:, :], in_=ident[:, :], compare_op=ALU.not_equal, fill=1.0, base=0,
                                    pattern=[[-1, 128]], channel_multiplier=1).then_inc(ready, 1)
            for k in range(2):
                v = before[:, k, 128 * k:128 * k + 128]
                nc.gpsimd.affine_select(out=v, in_=v, compare_op=ALU.is_gt, fill=0.0, base=0,
                                        pattern=[[-1, 128]], channel_multiplier=1).then_inc(ready, 1)
            nc.gpsimd.memset(before[:, 0, 128:256], 0.0).then_inc(ready, 1)
            nc.gpsimd.iota(dummy_i[:, :], [[0, 2], [128, 2]], base=DUMMY, channel_multiplier=1).then_inc(ready, 1)

            def gate(*waits):
                for s, v in waits:
                    wait_past(pool, s, v)
                pool.sem_inc(gates, 1)

            def edge_pass(e, of, tiles, rows_read, to, buf, target_set):
                def step(new, old):
                    for b in range(2):
                        if new and b == 0:
                            gate((e.gidx_ready, new.n + 1), (rows_read, new.n - 1))
                        if new:
                            for s in range(b * tiles // 2, (b + 1) * tiles // 2):
                                pool.indirect_dma_start(rows[:, new.slot, s, :], None, of,
                                                        bass.IndirectOffsetOnAxis(ap=gidx[:, new.slot, s:s + 1], axis=0))\
                                    .then_inc(e.gathered[new.slot], 16)
                        if old and b == 0:
                            gate((e.out_ready, old.n + 1), (e.sidx_ready, old.n + 1))
                        if old:
                            if b == 0 and isinstance(old.n, int) and old.n == 0:
                                for s, v in target_set:
                                    gate((s, v))
                            else:
                                gate((e.scattered, 64 * old.n + 32 * b))
                            for s in (2 * b, 2 * b + 1):
                                pool.indirect_dma_start(to, bass.IndirectOffsetOnAxis(ap=sidx[:, old.slot, s:s + 1], axis=0),
                                                        buf[:, old.slot, s, :], None, compute_op=ALU.add).then_inc(e.scattered, 16)
                turns(pool, EDGE_TURNS, SCATTER_LAG, step)

            edge_pass(mlp, x, 8, mlp.xn_ready, x1, mout, [(x1_set, 32)])
            gate((mlp.scattered, 64 * EDGE_TURNS))
            edge_pass(wag, x1, 4, wag.xn_ready, d1, dout, [(d1_zeroed, 16)])
            for u in range(2):
                gate((n_x2.stored[u], 48 * HALF_NODES))
            edge_pass(gc1, h2, 4, gc1.summed, s2, mout, [])
            for u in range(2):
                gate((n_gcn.stored[u], 32 * HALF_NODES))
            edge_pass(gc2, z2, 4, gc2.summed, t2, mout, [])
            for u in range(2):
                gate((n_x3.stored[u], 16 * HALF_NODES))
            edge_pass(gra, x3, 4, gra.xn_ready, s3, mout, [(s3_zeroed, 16)])

        @block.vector
        def _(dve):
            V = nc.vector
            V.memset(w_f[:, :], 0.0).then_inc(w_zeroed, 1)
            V.memset(src_f[:, EP // 128:], 0.0).then_inc(spare_set, 1)
            V.memset(dst_f[:, EP // 128:], 0.0).then_inc(spare_set, 1)
            V.memset(dout[:, :, :, :], 0.0).then_inc(tables_f, 1)
            dve.wait_ge(lists_in, 64)
            V.tensor_copy(list_f[:, :, :], list_i[:, :, :]).then_inc(lists_float, 1)
            dve.wait_ge(tables, 64)
            dve.wait_ge(ready, 7)
            V.tensor_copy(dummy_f[:, :], dummy_i[:, :]).then_inc(tables_f, 1)
            dve.wait_ge(tables_f, 2)
            dve.wait_ge(loads, 16 * n_const)
            dve.wait_ge(wT_psum, 1)
            V.tensor_copy(l1wT[:, :], bank[0][:, 0:128]).then_inc(wT_out, 1)

            def cols(t, n):
                return t[:, bass.ds(n * 4, 4)]

            def copy_cols(to, of):
                return V.tensor_scalar(to, of, 1.0, None, ALU.mult)

            def set_gidx(e, n, slot, tabs):
                for j, tab in enumerate(tabs):
                    ins = V.tensor_scalar(gidx[:, slot, 4 * j:4 * j + 4], cols(tab, n), float(N - 1), None, ALU.min)
                ins.then_inc(e.gidx_ready, 1)

            def set_next_gidx(e, new, tabs):
                wait_past(dve, e.gathered[1 - new.slot], 64 * len(tabs) * (new.use + new.slot))
                set_gidx(e, new.n + 1, 1 - new.slot, tabs)

            def row_stats(steps, slot, count, rows_of, between=None):
                for s in range(count):
                    steps.inc(V.bn_stats(stats[:, s, :], rows_of(s)))
                steps.wait()
                if between:
                    between()
                for s in range(count):
                    ins = V.bn_aggr(mv[:, slot, s, :], stats[:, s, :])
                return ins

            def inverse(steps, slot, count, to):
                steps.inc(V.reciprocal(to[:, slot, 0:count], sd[:, slot, 0:count]))
                steps.wait()

            def minus_mean_rstd(slot, count):
                return V.scalar_tensor_tensor(out=nmr[:, slot, 0:count], in0=mv[:, slot, 0:count, 0], scalar=-1.0,
                                              in1=rstd[:, slot, 0:count], op0=ALU.mult, op1=ALU.mult)

            def idx_view(new, s):
                b = s // 2
                return idx_row[:, new.slot, 256 * b:256 * b + 256].rearrange("q (p k) -> q k p", k=2)

            def by_k(t):
                return t.rearrange("q (k p) -> q k p", k=2)

            def equalities(new, weight=None):
                for s in range(4):
                    w = (weight[:, new.slot, s:s + 1], ALU.is_equal, ALU.mult) if weight is not None else (None, ALU.is_equal)
                    ins = V.tensor_scalar(by_k(eq[:, new.slot, s, :]), idx_view(new, s), key[:, new.slot, s:s + 1], *w)
                return ins

            def leaders(steps, new, to):
                for s in range(4):
                    steps.inc(V.scalar_tensor_tensor(out=by_k(junk[:, s, :]), in0=idx_view(new, s), scalar=key[:, new.slot, s:s + 1],
                                                     in1=by_k(before[:, s % 2, :]), op0=ALU.is_equal, op1=ALU.mult,
                                                     accum_out=cnt[:, s:s + 1]))
                steps.inc(V.tensor_tensor(off[:, :], dummy_f[:, :], key[:, new.slot, :], ALU.subtract))
                steps.wait()
                steps.inc(V.scalar_tensor_tensor(out=off2[:, :], in0=cnt[:, :], scalar=1.0, in1=off[:, :], op0=ALU.min, op1=ALU.mult))
                steps.wait()
                return V.tensor_tensor(to, off2[:, :], key[:, new.slot, :], ALU.add)

            steps = Steps(dve, mlp.dve, 8 + 1 + 1 + 6)
            set_gidx(mlp, 0, 0, (src_f, dst_f))

            def mlp_step(new, old):
                if new:
                    steps.begin(new)
                    set_next_gidx(mlp, new, (src_f, dst_f))
                    dve.wait_ge(mlp.gathered[new.slot], 128 * (new.use + 1))
                    row_stats(steps, new.slot, 8, lambda s: rows[:, new.slot, s, :],
                              lambda: steps.inc(copy_cols(key[:, new.slot, :], cols(src_f, new.n)))).then_inc(mlp.var_ready, 1)
                    steps.wait()
                    dve.wait_ge(mlp.row_loaded[new.slot], 16 * (new.use + 1))
                    wait_past(dve, mlp.summed, new.n - 1)
                    equalities(new).then_inc(mlp.eq_ready, 1)
                    dve.wait_ge(mlp.sd_ready, new.n + 1)
                    inverse(steps, new.slot, 8, rstd)
                    minus_mean_rstd(new.slot, 8).then_inc(mlp.norm_ready, 1)
                    wait_past(dve, mlp.scattered, 64 * (new.n - 1))
                    leaders(steps, new, sidx[:, new.slot, :]).then_inc(mlp.sidx_ready, 1)
                    dve.wait_ge(mlp.sidx_ready, new.n + 1)
                    dve.sem_inc(mlp.row_read, 1)
                    steps.end()
                if old:
                    dve.wait_ge(msg_psum, old.n + 1)
                    V.tensor_tensor(msg[:, :, :], by4(bank[5][:, :]), row4(b2r), ALU.add).then_inc(msg_out, 1)

            turns(dve, EDGE_TURNS, 1, mlp_step)

            wsteps = Steps(dve, wag.dve, 4 + 2 + 1 + 4 + 6)
            dve.wait_ge(mlp.scattered, 64 * EDGE_TURNS)
            set_gidx(wag, 0, 0, (src_f,))

            def wag_step(new, old):
                wsteps.begin(new)
                set_next_gidx(wag, new, (src_f,))
                dve.wait_ge(wag.gathered[new.slot], 64 * (new.use + 1))

                def keys():
                    wsteps.inc(copy_cols(key[:, new.slot, :], cols(dst_f, new.n)))
                    wsteps.inc(copy_cols(wkey[:, new.slot, :], cols(w_f, new.n)))
                row_stats(wsteps, new.slot, 4, lambda s: rows[:, new.slot, s, :], keys).then_inc(wag.var_ready, 1)
                wsteps.wait()
                dve.wait_ge(wag.row_loaded[new.slot], 16 * (new.use + 1))
                wait_past(dve, wag.summed, new.n - 1)
                equalities(new, wkey).then_inc(wag.eq_ready, 1)
                dve.wait_ge(wag.sd_ready, new.n + 1)
                inverse(wsteps, new.slot, 4, rstd)
                minus_mean_rstd(new.slot, 4).then_inc(wag.norm_ready, 1)
                wait_past(dve, wag.scattered, 64 * (new.n - 1))
                for s in range(4):
                    wsteps.inc(V.tensor_scalar(by_k(junk[:, s, :]), idx_view(new, s), key[:, new.slot, s:s + 1], 0.0,
                                               ALU.is_equal, ALU.add, accum_out=dout[:, new.slot, s, D:D + 1]))
                wsteps.wait()
                leaders(wsteps, new, sidx[:, new.slot, :]).then_inc(wag.sidx_ready, 1)
                dve.wait_ge(wag.sidx_ready, new.n + 1)
                copy_cols(cols(leader, new.n), sidx[:, new.slot, :]).then_inc(wag.row_read, 1)
                wsteps.end()

            turns(dve, EDGE_TURNS, 0, wag_step)

            xsteps = Steps(dve, n_x2.dve, 1 + 4)
            xsteps2 = Steps(dve, x2_norm_steps, 3)

            def x2_step(new, old):
                if new:
                    xsteps.begin(new)
                    dve.wait_ge(n_x2.loaded[new.slot], 32 * (new.use + 1))
                    xsteps.inc(V.tensor_tensor(by4(tmp[:, 0, :]), by4(na[:, new.slot, :]), row4(l1b), ALU.add))
                    xsteps.wait()
                    wait_past(dve, n_x2.stored[new.slot], 48 * new.use)
                    V.tensor_tensor(by4(nt[:, new.slot, :]), by4(tmp[:, 0, :]), by4(nb[:, new.slot, :])[:, :, 0:D], ALU.add)\
                        .then_inc(x2_ready, 1)
                    dve.wait_ge(x2_ready, new.n + 1)
                    row_stats(xsteps, new.slot, 4, lambda s: nt[:, new.slot, 128 * s:128 * s + 128],
                              lambda: V.tensor_copy(degree[:, new.slot, :], by4(nb[:, new.slot, :])[:, :, D])).then_inc(n_x2.inputs_read, 1)
                    xsteps.end()
                if old:
                    xsteps2.begin(old)
                    dve.wait_ge(sd_ready, old.n + 1)
                    inverse(xsteps2, old.slot, 8, rsd)
                    xsteps2.inc(V.tensor_tensor(rstd[:, old.slot, 0:4], rsd[:, old.slot, 0:4], rsd[:, old.slot, 4:8], ALU.mult))
                    xsteps2.inc(copy_cols(cols(dinv, old.n), rsd[:, old.slot, 4:8]))
                    xsteps2.wait()
                    minus_mean_rstd(old.slot, 4).then_inc(x2_norm, 1)
                    xsteps2.end()

            turns(dve, NODE_TURNS, 1, x2_step)

            def plain_edges(e, source_read):
                psteps = Steps(dve, e.dve, 1 + (5 if source_read else 0))
                set_gidx(e, 0, 0, (src_f,))

                def step(new, old):
                    psteps.begin(new)
                    set_next_gidx(e, new, (src_f,))
                    def keys():
                        psteps.inc(copy_cols(key[:, new.slot, :], cols(dst_f, new.n)))
                    if source_read:
                        dve.wait_ge(e.gathered[new.slot], 64 * (new.use + 1))
                        row_stats(psteps, new.slot, 4, lambda s: rows[:, new.slot, s, :], keys).then_inc(e.var_ready, 1)
                    else:
                        keys()
                    dve.wait_ge(e.row_loaded[new.slot], 16 * (new.use + 1))
                    wait_past(dve, e.summed, new.n - 1)
                    psteps.wait()
                    equalities(new).then_inc(e.eq_ready, 1)
                    if source_read:
                        dve.wait_ge(e.sd_ready, new.n + 1)
                        inverse(psteps, new.slot, 4, rstd)
                        minus_mean_rstd(new.slot, 4).then_inc(e.norm_ready, 1)
                    wait_past(dve, e.scattered, 64 * (new.n - 1))
                    copy_cols(sidx[:, new.slot, :], cols(leader, new.n)).then_inc(e.sidx_ready, 1)
                    dve.wait_ge(e.eq_ready, new.n + 1)
                    dve.sem_inc(e.row_read, 1)
                    psteps.end()

                turns(dve, EDGE_TURNS, 0, step)

            dve.wait_ge(wag.scattered, 64 * EDGE_TURNS)
            plain_edges(gc1, False)

            def gcn_step(new, old):
                if new:
                    dve.wait_ge(n_gcn.loaded[new.slot], 16 * (new.use + 1))
                    wait_past(dve, n_gcn.turned, new.n - 1)
                    V.tensor_tensor(by4(nt[:, new.slot, :]), by4(na[:, new.slot, :]), dinv4(new.n), ALU.mult)\
                        .then_inc(n_gcn.inputs_read, 1)
                if old:
                    if old.before():
                        z_out(old.before())
                    for c in (2, 3):
                        dve.wait_ge(ghid_psum, 4 * old.n + c + 1)
                        V.tensor_scalar(hid[:, c, :], bank[1 + c][:, :], gb1[:, c:c + 1], 0.0, ALU.add, ALU.max)\
                            .then_inc(ghid_dve, 1)

            def z_out(t):
                dve.wait_ge(n_gcn.product, t.n + 1)
                wait_past(dve, n_gcn.stored[t.slot], 32 * t.use)
                V.tensor_tensor(by4(no[:, t.slot, :]), by4(bank[5][:, :]), dinv4(t.n), ALU.mult).then_inc(n_gcn.result, 1)

            turns(dve, NODE_TURNS, 1, gcn_step)
            z_out(Turn(NODE_TURNS - 1, 1, HALF_NODES - 1))

            dve.wait_ge(gc1.scattered, 64 * EDGE_TURNS)
            plain_edges(gc2, False)

            x3steps = Steps(dve, n_x3.dve, 2)

            def x3_step(new, old):
                x3steps.begin(new)
                dve.wait_ge(n_x3.loaded[new.slot], 32 * (new.use + 1))
                x3steps.inc(V.tensor_tensor(by4(tmp[:, 0, :]), by4(nb[:, new.slot, 0:512]), dinv4(new.n), ALU.mult))
                x3steps.wait()
                x3steps.inc(V.tensor_tensor(by4(tmp[:, 1, :]), by4(tmp[:, 0, :]), row4(gb2), ALU.add))
                x3steps.wait()
                wait_past(dve, n_x3.stored[new.slot], 16 * new.use)
                V.scalar_tensor_tensor(out=no[:, new.slot, :], in0=tmp[:, 1, :], scalar=0.0, in1=na[:, new.slot, :],
                                       op0=ALU.max, op1=ALU.add).then_inc(n_x3.result, 1)
                x3steps.end()

            turns(dve, NODE_TURNS, 0, x3_step)

            dve.wait_ge(gc2.scattered, 64 * EDGE_TURNS)
            plain_edges(gra, True)

            osteps = Steps(dve, n_out.dve, 1)

            def out_step(new, old):
                osteps.begin(new)
                dve.wait_ge(n_out.product, new.n + 1)
                osteps.inc(V.tensor_tensor(by4(tmp[:, 0, :]), by4(bank[1][:, :]), row4(l3b), ALU.add))
                osteps.wait()
                wait_past(dve, n_out.stored[new.slot], 16 * new.use)
                V.scalar_tensor_tensor(out=no[:, new.slot, :], in0=tmp[:, 0, :], scalar=0.0, in1=na[:, new.slot, :],
                                       op0=ALU.max, op1=ALU.add).then_inc(n_out.result, 1)
                osteps.end()

            turns(dve, NODE_TURNS, 0, out_step)

        @block.scalar
        def _(act):
            S = nc.scalar
            act.dma_start(x1[0:N, :].rearrange("(a r) f -> a (r f)", a=800), x.rearrange("(a r) f -> a (r f)", a=800)).then_inc(x1_set, 16)
            act.wait_ge(zero_ready, 2)
            act.dma_start(x1[N:NP, :].rearrange("(p r) f -> p (r f)", p=88), zero[0:88, 0:4 * D]).then_inc(x1_set, 16)
            for to, w, s in ((d1, DW, d1_zeroed), (s3, D, s3_zeroed)):
                act.dma_start(to.rearrange("(p c r) f -> p c (r f)", p=128, r=8),
                              zero[:, 0:8 * w].rearrange("p (a j) -> p a j", a=1).to_broadcast([128, NP // 1024, 8 * w])).then_inc(s, 16)
            act.wait_ge(loads, 16 * n_const)

            def normalise(e, new, count, func):
                act.wait_ge(e.var_ready, new.n + 1)
                S.activation(sd[:, new.slot, 0:count], mv[:, new.slot, 0:count, 1], ACT.Sqrt, bias=eps_c[:, :]).then_inc(e.sd_ready, 1)
                act.wait_ge(e.norm_ready, new.n + 1)
                for s in range(count):
                    ins = S.activation(xn[:, s, :], rows[:, new.slot, s, :], func, bias=nmr[:, new.slot, s:s + 1],
                                       scale=rstd[:, new.slot, s:s + 1])
                ins.then_inc(e.xn_ready, 1)

            def sums_out(e, t, of, to):
                act.wait_ge(e.summed, t.n + 1)
                wait_past(act, e.scattered, 64 * (t.n - 1))
                S.activation(to[:, t.slot, :, 0:D], by4(of[:, :]), ACT.Copy).then_inc(e.out_ready, 1)

            def mlp_step(new, old):
                if old:
                    for j, (to, of, func) in enumerate(((hTs, bank[0], ACT.Relu), (hTd, bank[1], ACT.Relu), (eT, bank[2], ACT.Copy))):
                        act.wait_ge(turned, 3 * old.n + j + 1)
                        p = 64 if j == 2 else 128
                        S.activation(to[:, :], of[0:p, :], func).then_inc(turned_out, 1)
                if new:
                    normalise(mlp, new, 8, ACT.Identity)
                if old:
                    for c in range(2):
                        act.wait_ge(hid_psum, 2 * old.n + c + 1)
                        S.activation(hid[:, c, :], bank[3 + c][:, :], ACT.Relu, bias=b1c[:, c:c + 1]).then_inc(hid_out, 1)
                    sums_out(mlp, old, bank[6], mout)

            turns(act, EDGE_TURNS, 1, mlp_step)

            def wag_step(new, old):
                if old:
                    act.wait_ge(aggT_psum, old.n + 1)
                    S.activation(hTs[:, :], bank[0][:, :], ACT.Copy).then_inc(aggT_out, 1)
                if new:
                    normalise(wag, new, 4, ACT.Relu)
                if old:
                    sums_out(wag, old, bank[1], dout)

            turns(act, EDGE_TURNS, 1, wag_step)

            def h2_step(new, old):
                if new:
                    act.wait_ge(n_x2.inputs_read, new.n + 1)
                    S.activation(sd[:, new.slot, 0:4], mv[:, new.slot, 0:4, 1], ACT.Sqrt, bias=eps_c[:, :])
                    S.activation(sd[:, new.slot, 4:8], degree[:, new.slot, :], ACT.Sqrt, bias=1.0).then_inc(sd_ready, 1)
                if old:
                    act.wait_ge(x2_norm, old.n + 1)
                    wait_past(act, n_x2.stored[old.slot], 48 * old.use)
                    for s in range(4):
                        f = slice(128 * s, 128 * s + 128)
                        ins = S.activation(no[:, old.slot, f], nt[:, old.slot, f], ACT.Relu, bias=nmr[:, old.slot, s:s + 1],
                                           scale=rstd[:, old.slot, s:s + 1])
                    ins.then_inc(n_x2.result, 1)

            turns(act, NODE_TURNS, 1, h2_step)

            def plain_out(e):
                def step(new, old):
                    for slot in range(2):
                        if new.slot == slot:
                            sums_out(e, new, bank[6 + slot], mout)
                turns(act, EDGE_TURNS, 0, step)

            plain_out(gc1)

            def gcn_step(new, old):
                act.wait_ge(n_gcn.turned, new.n + 1)
                S.activation(hTs[:, :], bank[0][:, :], ACT.Copy).then_inc(n_gcn.turned_out, 1)
                for c in range(2):
                    act.wait_ge(ghid_psum, 4 * new.n + c + 1)
                    S.activation(hid[:, c, :], bank[1 + c][:, :], ACT.Relu, bias=gb1[:, c:c + 1]).then_inc(ghid_act, 1)

            turns(act, NODE_TURNS, 0, gcn_step)

            plain_out(gc2)

            def gra_step(new, old):
                if new:
                    wait_past(act, gra.summed, new.n)
                    normalise(gra, new, 4, ACT.Relu)
                if old:
                    sums_out(gra, old, bank[6], mout)

            turns(act, EDGE_TURNS, 1, gra_step)

            def out_step(new, old):
                act.wait_ge(n_out.turned, new.n + 1)
                S.activation(hid[:, new.slot, :], bank[0][:, :], ACT.Copy).then_inc(n_out.turned_out, 1)

            turns(act, NODE_TURNS, 0, out_step)

        @block.tensor
        def _(pe):
            T = nc.tensor
            pe.wait_ge(ready, 7)
            pe.wait_ge(loads, 16 * n_const)
            T.transpose(bank[0][:, 0:128], l1w[:, :], ident[:, :]).then_inc(wT_psum, 1)
            pe.wait_ge(wT_out, 1)

            def turn_rows(to, of, start=0):
                for s in range(4):
                    ins = T.transpose(to[:, 128 * s:128 * s + 128], of(s), ident[:, :])
                return ins

            def batch_sums(to, of, slot):
                for b in range(2):
                    for k2 in range(2):
                        s2 = 2 * b + k2
                        for k in range(2):
                            ins = T.matmul(to[:, 128 * s2:128 * s2 + 128], eq[:, slot, 2 * b + k, 128 * k2:128 * k2 + 128],
                                           of(2 * b + k), start=(k == 0), stop=(k == 1))
                return ins

            def mlp_step(t, _):
                uses = 16 * (t.use + 1) + (16 if isinstance(t.n, int) and t.n == EDGE_TURNS - 1 else 0)
                pe.wait_ge(ea_loaded[t.slot], uses)
                pe.wait_ge(mlp.xn_ready, t.n + 1)
                wait_past(pe, turned_out, 3 * t.n)
                turn_rows(bank[0], lambda s: xn[:, s, :]).then_inc(turned, 1)
                turn_rows(bank[1], lambda s: xn[:, 4 + s, :]).then_inc(turned, 1)
                for s in range(4):
                    ins = T.transpose(bank[2][0:64, 128 * s:128 * s + 128], eav[:, t.slot, s, :], ident[:, :])
                ins.then_inc(turned, 1)
                pe.wait_ge(turned_out, 3 * t.n + 3)
                wait_past(pe, hid_out, 2 * t.n)
                for c in range(2):
                    f = slice(128 * c, 128 * c + 128)
                    T.matmul(bank[3 + c][:, :], w1s[:, f], hTs[:, :], start=True, stop=False)
                    T.matmul(bank[3 + c][:, :], w1d[:, f], hTd[:, :], start=False, stop=False)
                    T.matmul(bank[3 + c][:, :], w1e[:, f], eT[:, :], start=False, stop=True).then_inc(hid_psum, 1)
                pe.wait_ge(hid_out, 2 * t.n + 2)
                wait_past(pe, msg_out, t.n)
                for s in range(4):
                    f = slice(128 * s, 128 * s + 128)
                    for c in range(2):
                        ins = T.matmul(bank[5][:, f], hid[:, c, f], w2c[:, c, :], start=(c == 0), stop=(c == 1))
                ins.then_inc(msg_psum, 1)
                pe.wait_ge(msg_out, t.n + 1)
                pe.wait_ge(mlp.eq_ready, t.n + 1)
                wait_past(pe, mlp.out_ready, t.n)
                batch_sums(bank[6], lambda s: msg[:, s, :], t.slot).then_inc(mlp.summed, 1)

            turns(pe, EDGE_TURNS - 1, 0, mlp_step)
            mlp_step(Turn(EDGE_TURNS - 1, (EDGE_TURNS - 1) % 2, (EDGE_TURNS - 1) // 2), None)

            def wag_step(t, _):
                pe.wait_ge(wag.xn_ready, t.n + 1)
                pe.wait_ge(wag.eq_ready, t.n + 1)
                wait_past(pe, aggT_out, t.n)
                for b in range(2):
                    for k in range(2):
                        s = 2 * b + k
                        ins = T.matmul(bank[0][:, 256 * b:256 * b + 256], xn[:, s, :], eq[:, t.slot, s, :],
                                       start=(k == 0), stop=(k == 1))
                ins.then_inc(aggT_psum, 1)
                pe.wait_ge(aggT_out, t.n + 1)
                wait_past(pe, wag.out_ready, t.n)
                for s in range(4):
                    f = slice(128 * s, 128 * s + 128)
                    ins = T.matmul(bank[1][:, f], hTs[:, f], l1wT[:, :], start=True, stop=True)
                ins.then_inc(wag.summed, 1)

            turns(pe, EDGE_TURNS, 0, wag_step)

            def plain_sums(e):
                def step(t, _):
                    pe.wait_ge(e.gathered[t.slot], 64 * (t.use + 1))
                    pe.wait_ge(e.eq_ready, t.n + 1)
                    wait_past(pe, e.out_ready, t.n - 1)
                    batch_sums(bank[6 + t.slot], lambda s: rows[:, t.slot, s, :], t.slot).then_inc(e.summed, 1)
                turns(pe, EDGE_TURNS, 0, step)

            plain_sums(gc1)

            def second(t):
                pe.wait_ge(ghid_act, 2 * t.n + 2)
                pe.wait_ge(ghid_dve, 2 * t.n + 2)
                wait_past(pe, n_gcn.result, t.n)
                for s in range(4):
                    f = slice(128 * s, 128 * s + 128)
                    for c in range(4):
                        ins = T.matmul(bank[5][:, f], hid[:, c, f], gw2[:, c, :], start=(c == 0), stop=(c == 3))
                ins.then_inc(n_gcn.product, 1)

            def gcn_step(new, old):
                if new:
                    pe.wait_ge(n_gcn.inputs_read, new.n + 1)
                    wait_past(pe, n_gcn.turned_out, new.n)
                    turn_rows(bank[0], lambda s: nt[:, new.slot, 128 * s:128 * s + 128]).then_inc(n_gcn.turned, 1)
                if old:
                    second(old)
                if new:
                    pe.wait_ge(n_gcn.turned_out, new.n + 1)
                    for c in range(4):
                        T.matmul(bank[1 + c][:, :], gw1[:, 128 * c:128 * c + 128], hTs[:, :], start=True, stop=True)\
                            .then_inc(ghid_psum, 1)

            turns(pe, NODE_TURNS, 1, gcn_step)

            plain_sums(gc2)

            def gra_step(t, _):
                pe.wait_ge(gra.xn_ready, t.n + 1)
                pe.wait_ge(gra.eq_ready, t.n + 1)
                wait_past(pe, gra.out_ready, t.n)
                batch_sums(bank[6], lambda s: xn[:, s, :], t.slot).then_inc(gra.summed, 1)

            turns(pe, EDGE_TURNS, 0, gra_step)

            def out_step(new, old):
                if new:
                    pe.wait_ge(n_out.loaded[new.slot], 32 * (new.use + 1))
                    wait_past(pe, n_out.turned_out, new.n)
                    turn_rows(bank[0], lambda s: nb[:, new.slot, 128 * s:128 * s + 128]).then_inc(n_out.turned, 1)
                if old:
                    pe.wait_ge(n_out.turned_out, old.n + 1)
                    wait_past(pe, n_out.result, old.n)
                    for s in range(4):
                        f = slice(128 * s, 128 * s + 128)
                        ins = T.matmul(bank[1][:, f], hid[:, old.slot, f], l3w[:, :], start=True, stop=True)
                    ins.then_inc(n_out.product, 1)

            turns(pe, NODE_TURNS, 1, out_step)


_INS = ["x", "src", "dst", "edge_attr_64", "edge_weight", "L0_gnn_W1", "L0_gnn_b1", "L0_gnn_W2", "L0_gnn_b2", "L1_gnn_W",
        "L1_gnn_b", "L2_gnn_W1", "L2_gnn_b1", "L2_gnn_W2", "L2_gnn_b2", "L3_gnn_W", "L3_gnn_b"]


def kernel(**inputs):
    import numpy as _np
    import concourse.bacc as _bacc
    from concourse import mybir as _mybir
    from concourse.bass_utils import run_bass_kernel_spmd as _run

    nc = _bacc.Bacc("TRN2", target_bir_lowering=False, num_devices=1)
    arrays, args = {}, []
    for name in _INS:
        a = _np.ascontiguousarray(inputs[name])
        arrays[f"in_{name}_dram"] = a
        args.append(nc.dram_tensor(f"in_{name}_dram", a.shape, _mybir.dt.from_np(a.dtype), kind="ExternalInput").ap())
    args.append(nc.dram_tensor("out_0_dram", (N, D), _mybir.dt.float32, kind="ExternalOutput").ap())
    build(nc, *args)
    r = _run(nc, [arrays], core_ids=[0])
    return r.results[0]["out_0_dram"]
```

```python
import concourse.bass as bass
from concourse import mybir
from contextlib import ExitStack

F32 = mybir.dt.float32
I32 = mybir.dt.int32
ALU = mybir.AluOpType
ACT = mybir.ActivationFunctionType
AX = mybir.AxisListType

D = 128
N = 100000
E = 50000
NODE_TURNS = -(-N // 512)
NP = NODE_TURNS * 512
EDGE_TURNS = -(-E // 512)
EP = EDGE_TURNS * 512
DUMMY = NP
NR = NP + 512
PAD_INDEX = N
DW = D + 4
LATER = 1024.0
EPS = 1e-5
WINDOW = 2
DELAY = WINDOW + 6
assert NODE_TURNS == 2 * EDGE_TURNS and NODE_TURNS % 4 == 0 and NP == 1024 * EDGE_TURNS
assert E % 2 == 0 and PAD_INDEX < NP


class Turn:

    def __init__(self, i, const, stride=0):
        self.i, self.const, self.stride = i, const, stride
        self.n = const if i is None else i * stride + const

    def slot(self, d=2):
        assert self.stride % d == 0
        return self.const % d

    def use(self, d=2):
        return self.const // d if self.i is None else i_times(self.i, self.stride // d) + self.const // d

    def first(self):
        return self.i is None and self.const == 0


def i_times(i, k):
    return i if k == 1 else i * k


class Part:

    def __init__(self, count, lag, step, per=1, delay=0):
        self.count, self.lag, self.step, self.per, self.delay = count, lag, step, per, delay

    def run(self, turn, i=None, unroll=0):
        for j in range(self.per):
            const = self.per * (turn - self.delay) + j
            stride = self.per * unroll

            def at(k, const=const, stride=stride):
                if i is None and not 0 <= const - k < self.count:
                    return None
                return Turn(i, const - k, stride)

            if i is not None or 0 <= const < self.count + self.lag:
                self.step(at)


def run(eng, parts, oldest=4):
    unroll = 4 if len(parts) == 1 and parts[0].count == NODE_TURNS else 2
    first = max(p.delay + -(-(p.lag + oldest) // p.per) for p in parts)
    end = min(p.delay + p.count // p.per for p in parts)
    first += (end - first) % unroll
    last = max(p.delay + -(-(p.count + p.lag) // p.per) for p in parts)
    for c in range(first):
        for p in parts:
            p.run(c)
    with eng.Fori(0, (end - first) // unroll) as i:
        for u in range(unroll):
            for p in parts:
                p.run(first + u, i, unroll)
    for c in range(end, last):
        for p in parts:
            p.run(c)


def wait_past(eng, sem, value):
    if not isinstance(value, int) or value > 0:
        eng.wait_ge(sem, value)


class Steps:

    def __init__(self, eng, sem, per_turn):
        self.eng, self.sem, self.per_turn, self.turn, self.done = eng, sem, per_turn, None, 0

    def begin(self, turn):
        self.turn, self.done = turn, 0

    def inc(self, instruction):
        self.done += 1
        instruction.then_inc(self.sem, 1)

    def wait(self):
        self.eng.wait_ge(self.sem, self.turn.n * self.per_turn + self.done)

    def end(self):
        assert self.done == self.per_turn, (self.done, self.per_turn)


def build(nc, x, src, dst, ea, ew, m1_w1, m1_b1, m1_w2, m1_b2, l1_w, l1_b, g_w1, g_b1, g_w2, g_b2, l3_w, l3_b, out):
    ctx = ExitStack()

    def sb(name, shape, dt=F32):
        return ctx.enter_context(nc.sbuf_tensor(name, shape, dt))

    def sem(name):
        return ctx.enter_context(nc.semaphore(name))

    def dram(name, shape, dt=F32):
        return nc.dram_tensor(name, shape, dt, kind="Internal").ap()

    with ctx:
        src_pad = dram("src_pad", [EP])
        dst_pad = dram("dst_pad", [EP])
        x1 = dram("x1", [NR, D])
        d1 = dram("d1", [NR, DW])
        x2 = dram("x2", [NP, D])
        h2 = dram("h2", [NP, D])
        s2 = dram("s2", [NR, D])
        z2 = dram("z2", [NP, D])
        t2 = dram("t2", [NR, D])
        x3 = dram("x3", [NP, D])
        s3 = dram("s3", [NR, D])

        ident = sb("ident", [128, 128])
        rank = sb("rank", [128, 4, 512])
        dummy_i = sb("dummy_i", [128, 4], I32)
        dummy_f = sb("dummy_f", [128, 4])
        even_i = sb("even_i", [128, EP // 128], I32)
        dev = sb("dev", [128, EP // 128])
        lag_col = sb("lag_col", [128, 1])
        lag_min = sb("lag_min", [1, 1])
        ascends = sb("ascends", [1, 1], I32)
        zero = sb("zero", [128, 8 * D])
        d1_row = sb("d1_row", [128, 8, DW])
        eps_c = sb("eps_c", [128, 1])
        list_i = sb("list_i", [112, 2, EP // 112], I32)
        list_f = sb("list_f", [112, 2, EP // 112])
        w1s, w1d = sb("w1s", [128, 256]), sb("w1d", [128, 256])
        w1e = sb("w1e", [64, 256])
        b1c = sb("b1c", [128, 2])
        w2c = sb("w2c", [128, 2, 128])
        b2r = sb("b2r", [128, 128])
        l1w = sb("l1w", [128, 128])
        l1wT = sb("l1wT", [128, 128])
        l1b = sb("l1b", [128, 128])
        gw1 = sb("gw1", [128, 512])
        gb1 = sb("gb1", [128, 4])
        gw2 = sb("gw2", [128, 4, 128])
        gb2 = sb("gb2", [128, 128])
        l3w = sb("l3w", [128, 128])
        l3b = sb("l3b", [128, 128])
        src_f = sb("src_f", [128, EP // 128 + 4])
        dst_f = sb("dst_f", [128, EP // 128 + 4])
        w_f = sb("w_f", [128, EP // 128])
        leader = sb("leader", [128, EP // 128], I32)
        dinv = sb("dinv", [128, 4 * NODE_TURNS])

        rows = sb("rows", [128, 2, 8, 128])
        xn = sb("xn", [128, 8, 128])
        xw = sb("xw", [128, 4, 128])
        eav = sb("eav", [128, 2, 4, 64])
        idx_row = sb("idx_row", [128, 2, 512])
        key = sb("key", [128, 2, 4])
        gidx = sb("gidx", [128, 2, 8], I32)
        sidx = sb("sidx", [128, 2, 4], I32)
        eq = sb("eq", [128, 2, 4, 512])
        junk = sb("junk", [128, 4, 512])
        stats = sb("stats", [128, 8, 6])
        mv = sb("mv", [128, 2, 8, 2])
        sd = sb("sd", [128, 2, 8])
        rstd = sb("rstd", [128, 2, 8])
        nmr = sb("nmr", [128, 2, 8])
        cnt = sb("cnt", [128, 4])
        off = sb("off", [128, 4])
        off2 = sb("off2", [128, 4])
        hTs, hTd = sb("hTs", [128, 512]), sb("hTd", [128, 512])
        eT = sb("eT", [64, 512])
        ehid = sb("ehid", [128, 2, 512])
        msg = sb("msg", [128, 4, 128])
        mout = sb("mout", [128, 2, 4, 128])
        dout = sb("dout", [128, 2, 4, DW])

        na = sb("na", [128, 4, 512])
        nb = sb("nb", [128, 4, 4 * DW])
        nt = sb("nt", [128, 4, 512])
        no = sb("no", [128, 4, 512])
        ntmp = sb("ntmp", [128, 2, 512])
        nT = sb("nT", [128, 2, 512])
        nhid = sb("nhid", [128, 4, 512])
        nstats = sb("nstats", [128, 4, 6])
        nmv = sb("nmv", [128, 2, 4, 2])
        nsd = sb("nsd", [128, 2, 8])
        nrsd = sb("nrsd", [128, 2, 8])
        nrstd = sb("nrstd", [128, 2, 4])
        nnmr = sb("nnmr", [128, 2, 4])
        degree = sb("degree", [128, 2, 4])

        bank = [ctx.enter_context(nc.psum_tensor(f"bank{i}", [128, 512], F32)) for i in range(8)]

        zero_ready = sem("zero_set")
        d1_row_ready = sem("d1_row_set")
        ready = sem("constants_ready")
        loads = sem("constants_loaded")
        pad_ready = sem("pad_index_set")
        lists_in = sem("lists_in")
        lists_float = sem("lists_float")
        lists_out = sem("lists_out")
        spare_set = sem("spare_group_set")
        w_zeroed = sem("weights_zeroed")
        tables = sem("tables_loaded")
        x1_set = sem("x1_set")
        dummies_set = sem("dummy_rows_set")
        targets_set = sem("d1_and_s3_set")
        gates = sem("pool_gates")
        sp_gates = sem("sp_gates")
        tables_f = sem("tables_float")
        wT_psum = sem("l1_weight_transposed")
        wT_out = sem("l1_weight_copied")
        lag_ready = sem("dst_lag_ready")
        lag_psum = sem("dst_lag_transposed")
        flag_ready = sem("ascends_ready")

        class Edge:

            def __init__(self, tag, norm=True, lead=False):
                self.gidx_ready = sem(f"{tag}_gidx_ready")
                self.gathered = [sem(f"{tag}_gathered{u}") for u in range(2)]
                self.row_loaded = [sem(f"{tag}_idx_row_loaded{u}") for u in range(2)]
                self.row_read = sem(f"{tag}_idx_row_read")
                self.eq_ready = sem(f"{tag}_eq_ready")
                self.sidx_ready = sem(f"{tag}_sidx_ready")
                self.summed = sem(f"{tag}_summed")
                self.out_ready = sem(f"{tag}_out_ready")
                self.scattered = sem(f"{tag}_scattered")
                self.dve = sem(f"{tag}_dve_steps")
                if lead:
                    self.dve_lead = sem(f"{tag}_dve_leader_steps")
                if norm:
                    self.var_ready = sem(f"{tag}_var_ready")
                    self.sd_ready = sem(f"{tag}_sd_ready")
                    self.norm_ready = sem(f"{tag}_norm_ready")
                    self.xn_ready = sem(f"{tag}_xn_ready")

        node_loaded = [sem(f"node_loaded{u}") for u in range(4)]
        node_stored = [sem(f"node_stored{u}") for u in range(4)]

        class Node:

            def __init__(self, tag, loads, stores, after, own):
                self.loads, self.stores = 16 * loads, 16 * stores
                self.loads_before = after.loads_before + after.loads * NODE_TURNS // 4 if after else 0
                self.stores_before = after.stores_before + after.stores * NODE_TURNS // 4 if after else 0
                self.result = sem(f"{tag}_result")
                self.inputs_read = sem(f"{tag}_inputs_read") if "inputs" in own else self.result
                if "turn" in own:
                    self.turned = sem(f"{tag}_turned")
                    self.turned_out = sem(f"{tag}_turned_out")
                    self.product = sem(f"{tag}_product")
                if "dve" in own:
                    self.dve = sem(f"{tag}_dve_steps")

            def loaded(self, t):
                return self.loads_before + self.loads * (t.use(4) + 1)

            def slot_stored(self, t):
                return self.stores_before + self.stores * t.use(4)

        mlp, wag, gc1, gc2, gra = Edge("mlp", lead=True), Edge("wag", lead=True), Edge("gc1", norm=False), Edge("gc2", norm=False), Edge("gra")
        n_x2 = Node("n_x2", 2, 3, None, ("inputs", "dve"))
        n_gcn = Node("n_gcn", 1, 2, n_x2, ("inputs", "turn"))
        n_x3 = Node("n_x3", 2, 1, n_gcn, ("dve",))
        n_out = Node("n_out", 2, 1, n_x3, ("turn", "dve"))
        ea_loaded = [sem(f"ea_loaded{u}") for u in range(2)]
        turned = sem("mlp_turned")
        turned_out = sem("mlp_turned_out")
        hid_psum = sem("mlp_hidden")
        hid_out = sem("mlp_hidden_out")
        msg_psum = sem("mlp_messages")
        msg_out = sem("mlp_messages_out")
        xw_ready = sem("wag_weighted_rows")
        aggT_psum = sem("wag_sums_transposed")
        aggT_out = sem("wag_sums_copied")
        x2_ready = sem("x2_ready")
        x2_norm = sem("x2_norm_ready")
        x2_norm_steps = sem("x2_norm_steps")
        nsd_ready = sem("x2_sd_ready")
        ghid_psum = sem("gcn_hidden")
        ghid_act = sem("gcn_hidden_act")
        ghid_dve = sem("gcn_hidden_dve")

        ea_flat = ea.rearrange("e f -> (e f)")
        last_rows = N - (NODE_TURNS - 1) * 512
        full = (E // 256) * 256
        rest = (E - full) // 2
        n_const = 14

        def nodes(a, n, count=512):
            return a[bass.ds(n * 512, count), :].rearrange("(p k) f -> p (k f)", k=4)

        def by4(t):
            return t.rearrange("p (s f) -> p s f", s=4)

        def row4(t):
            return t[:, :].rearrange("p (a f) -> p a f", a=1).to_broadcast([128, 4, 128])

        def each4(t, n):
            return t[:, bass.ds(n * 4, 4)].rearrange("p (s a) -> p s a", a=1).to_broadcast([128, 4, 128])

        def last_turn(t):
            return t.i is None and t.n == EDGE_TURNS - 1

        def passes(eng, items):
            eng.wait_ge(flag_ready, 1)
            flag = eng.value_load(ascends[0:1, 0:1], min_val=0, max_val=1)

            def both(together):
                for prepare, edge, node in items:
                    prepare()
                    e = [Part(EDGE_TURNS, edge[1], edge[0])] if edge else []
                    nd = []
                    if node:
                        step = node[0](together)
                        nd = [Part(NODE_TURNS, node[1], step, 2 if together else 1, DELAY if together else 0)]
                    if together:
                        run(eng, e + nd)
                    else:
                        for part in e + nd:
                            run(eng, [part])

            with eng.If(flag == 1):
                both(True)
            with eng.Else():
                both(False)

        block = ctx.enter_context(nc.Block())

        @block.sync
        def _(sp):
            w = EP // 112
            sp.wait_ge(pad_ready, 1)
            for j, of in enumerate((src, dst)):
                sp.dma_start(list_i[0:E // w, j, :], of[0:E // w * w].rearrange("(a b) -> a b", b=w)).then_inc(lists_in, 16)
                sp.dma_start(list_i[E // w:E // w + 1, j, 0:E % w], of[E // w * w:E].rearrange("(a b) -> a b", a=1)).then_inc(lists_in, 16)
            consts = [(w1s[:, :], m1_w1[0:128, :]), (w1d[:, :], m1_w1[128:256, :]), (w1e[:, :], m1_w1[256:320, :]),
                      (w2c[:, :, :], m1_w2.rearrange("(c p) n -> p c n", p=128)), (l1w[:, :], l1_w), (gw1[:, :], g_w1),
                      (gw2[:, :, :], g_w2.rearrange("(c p) n -> p c n", p=128)), (l3w[:, :], l3_w)]
            consts += [(to[:, :], of.rearrange("(a n) -> a n", a=1).to_broadcast([128, 128]))
                       for to, of in ((b2r, m1_b2), (l1b, l1_b), (gb2, g_b2), (l3b, l3_b))]
            for to, of in consts:
                sp.dma_start(to, of).then_inc(loads, 16)
            with nc.allow_non_contiguous_dma(reason="bias vectors as columns, once"):
                sp.dma_start(b1c[:, :], m1_b1.rearrange("(c p) -> p c", p=128)).then_inc(loads, 16)
                sp.dma_start(gb1[:, :], g_b1.rearrange("(c p) -> p c", p=128)).then_inc(loads, 16)
            assert len(consts) + 2 == n_const
            sp.wait_ge(lists_float, 1)
            for j, to in enumerate((src_pad, dst_pad)):
                sp.dma_start(to.rearrange("(a b) -> a b", b=w), list_f[:, j, :]).then_inc(lists_out, 16)
            sp.wait_ge(lists_out, 32)
            sp.wait_ge(spare_set, 2)
            for tab, of in ((src_f, src_pad), (dst_f, dst_pad)):
                sp.dma_start(tab[:, 0:EP // 128].rearrange("p (c k) -> p c k", k=2),
                             of.rearrange("(c p k) -> p c k", p=128, k=2)).then_inc(tables, 16)
            sp.wait_ge(w_zeroed, 1)
            wv = w_f[:, :].rearrange("p (c k) -> p c k", k=2)
            sp.dma_start(wv[:, 0:full // 256, :], ew[0:full].rearrange("(c p k) -> p c k", p=128, k=2)).then_inc(tables, 16)
            sp.dma_start(wv[0:rest, full // 256, :], ew[full:E].rearrange("(p k) -> p k", k=2)).then_inc(tables, 16)
            sp.wait_ge(zero_ready, 2)
            for to, wd in ((x1, D), (d1, DW), (s2, D), (t2, D), (s3, D)):
                sp.dma_start(to[DUMMY:NR, :].rearrange("(p r) f -> p (r f)", r=4), zero[:, 0:4 * wd]).then_inc(dummies_set, 16)
            sp.wait_ge(d1_row_ready, 1)

            def load_idx_row(e, of, t):
                wait_past(sp, e.row_read, t.n - 1)
                sp.dma_start(idx_row[:, t.slot(), :], of[bass.ds(t.n * 512, 512)].rearrange("(a n) -> a n", a=1).to_broadcast([128, 512]))\
                    .then_inc(e.row_loaded[t.slot()], 16)

            def mlp_loads(at):
                t = at(0)
                load_idx_row(mlp, src_pad, t)
                wait_past(sp, turned, 3 * (t.n - 1))
                to = eav[:, t.slot(), :, :].rearrange("p (b k) f -> p b (k f)", k=2)
                if last_turn(t):
                    flat = ea_flat[t.n * 512 * 64:E * 64]
                    sp.dma_start(to[:, 0, :], flat[0:256 * 64].rearrange("(p j) -> p j", p=128)).then_inc(ea_loaded[t.slot()], 16)
                    sp.dma_start(to[0:rest, 1, :], flat[256 * 64:].rearrange("(p j) -> p j", p=rest)).then_inc(ea_loaded[t.slot()], 16)
                else:
                    of = ea_flat[bass.ds(t.n * (512 * 64), 512 * 64)]
                    sp.dma_start(to, of.rearrange("(b p j) -> p b j", b=2, p=128)).then_inc(ea_loaded[t.slot()], 16)
                for to, of in ((d1, d1_row[:, :, :].rearrange("p r f -> p (r f)")), (s3, zero[:, :])):
                    sp.dma_start(to[bass.ds(t.n * 1024, 1024), :].rearrange("(p r) f -> p (r f)", r=8), of).then_inc(targets_set, 16)

            run(sp, [Part(EDGE_TURNS - 1, 0, mlp_loads)])
            mlp_loads(lambda k: Turn(None, EDGE_TURNS - 1))

            def idx_rows(e):
                return lambda at: at(0) and load_idx_row(e, dst_pad, at(0))

            def row_slots_free(e):
                return lambda: sp.wait_ge(e.row_read, EDGE_TURNS)

            def node_io(s, sums, ins, outs):
                def steps(together):
                    def step(at):
                        new, old = at(0), at(4)
                        if new:
                            if together:
                                if new.i is None:
                                    need = min(new.n // 2 + WINDOW + 1, EDGE_TURNS)
                                else:
                                    need = i_times(new.i, new.stride // 2) + new.const // 2 + WINDOW + 1
                                sp.wait_ge(sums.scattered, 64 * need)
                                sp.sem_inc(sp_gates, 1)
                            elif new.first():
                                sp.wait_ge(sums.scattered, 64 * EDGE_TURNS)
                            wait_past(sp, s.inputs_read, new.n - 3)
                            for of, buf in ins:
                                sp.dma_start(buf[:, new.slot(4), 0:4 * of.shape[1]], nodes(of, new.n)).then_inc(node_loaded[new.slot(4)], 16)
                        if old:
                            for to, buf, result in outs:
                                sp.wait_ge(result, old.n + 1)
                                if to is out and old.i is None and old.n == NODE_TURNS - 1:
                                    sp.dma_start(nodes(out, old.n, last_rows), buf[0:last_rows // 4, old.slot(4), :]).then_inc(node_stored[old.slot(4)], 16)
                                else:
                                    sp.dma_start(nodes(to, old.n), buf[:, old.slot(4), :]).then_inc(node_stored[old.slot(4)], 16)
                    return step
                return steps, 4

            passes(sp, [
                (row_slots_free(mlp), (idx_rows(wag), 0),
                 node_io(n_x2, wag, [(x1, na), (d1, nb)], [(x2, nt, x2_ready), (h2, no, n_x2.result), (s2, no, n_x2.result)])),
                (row_slots_free(wag), (idx_rows(gc1), 0),
                 node_io(n_gcn, gc1, [(s2, na)], [(z2, no, n_gcn.result), (t2, no, n_gcn.result)])),
                (row_slots_free(gc1), (idx_rows(gc2), 0), node_io(n_x3, gc2, [(x2, na), (t2, nb)], [(x3, no, n_x3.result)])),
                (row_slots_free(gc2), (idx_rows(gra), 0), node_io(n_out, gra, [(x3, na), (s3, nb)], [(out, no, n_out.result)])),
            ])
            for u in range(4):
                sp.wait_ge(node_stored[u], n_out.stores_before + n_out.stores * (NODE_TURNS // 4))

        @block.gpsimd
        def _(pool):
            G = nc.gpsimd
            G.memset(list_i[:, :, :], PAD_INDEX).then_inc(pad_ready, 1)
            G.memset(zero[:, :], 0.0).then_inc(zero_ready, 1)
            G.memset(eps_c[:, :], EPS).then_inc(zero_ready, 1)
            G.memset(ident[:, :], 0.0).then_inc(ready, 1)
            G.memset(rank[:, :, :], 1.0).then_inc(ready, 1)
            pool.wait_ge(ready, 2)
            G.affine_select(out=ident[:, :], in_=ident[:, :], compare_op=ALU.not_equal, fill=1.0, base=0,
                            pattern=[[-1, 128]], channel_multiplier=1).then_inc(ready, 1)
            for s in range(4):
                place = dict(base=256 * (s // 2) + s % 2, pattern=[[-1, 512]], channel_multiplier=2)
                G.affine_select(out=rank[:, s, :], in_=rank[:, s, :], compare_op=ALU.is_ge, fill=LATER, **place).then_inc(ready, 1)
                pool.wait_ge(ready, 4 + 2 * s)
                G.affine_select(out=rank[:, s, :], in_=rank[:, s, :], compare_op=ALU.not_equal, fill=0.0, **place).then_inc(ready, 1)
            G.iota(dummy_i[:, :], [[128, 4]], base=DUMMY, channel_multiplier=1).then_inc(ready, 1)
            G.iota(even_i[:, :], [[512, EP // 256], [2, 2]], base=0, channel_multiplier=4).then_inc(ready, 1)

            def gate(*waits):
                for s, v in waits:
                    wait_past(pool, s, v)
                pool.sem_inc(gates, 1)

            def edge_step(e, of, tiles, rows_read, to, buf, lag, batches, target_set):
                def step(at):
                    new, old = at(0), at(lag)
                    for b in range(batches):
                        if new:
                            if b == 0:
                                gate((e.gidx_ready, new.n + 1), (rows_read, new.n - 1))
                            for s in range(b * tiles // batches, (b + 1) * tiles // batches):
                                pool.indirect_dma_start(rows[:, new.slot(), s, :], None, of,
                                                        bass.IndirectOffsetOnAxis(ap=gidx[:, new.slot(), s:s + 1], axis=0))\
                                    .then_inc(e.gathered[new.slot()], 16)
                        if old:
                            if b == 0:
                                gate((e.out_ready, old.n + 1), (e.sidx_ready, old.n + 1))
                            if b == 0 and old.first():
                                for s, v in target_set:
                                    gate((s, v))
                            else:
                                gate((e.scattered, 64 * old.n + 64 // batches * b))
                            for s in range(b * 4 // batches, (b + 1) * 4 // batches):
                                pool.indirect_dma_start(to, bass.IndirectOffsetOnAxis(ap=sidx[:, old.slot(), s:s + 1], axis=0),
                                                        buf[:, old.slot(), s, :], None, compute_op=ALU.add).then_inc(e.scattered, 16)
                return step, lag

            step, lag = edge_step(mlp, x, 8, mlp.xn_ready, x1, mout, 5, 2, [(x1_set, 32), (dummies_set, 80)])
            run(pool, [Part(EDGE_TURNS, lag, step)])

            def whole(s):
                def wait():
                    for u in range(4):
                        gate((node_stored[u], s.stores_before + s.stores * (NODE_TURNS // 4)))
                return wait

            passes(pool, [
                (lambda: gate((mlp.scattered, 64 * EDGE_TURNS)),
                 edge_step(wag, x1, 4, wag.xn_ready, d1, dout, 3, 1, [(targets_set, 32 * EDGE_TURNS)]), None),
                (whole(n_x2), edge_step(gc1, h2, 4, gc1.summed, s2, mout, 3, 1, []), None),
                (whole(n_gcn), edge_step(gc2, z2, 4, gc2.summed, t2, mout, 3, 1, []), None),
                (whole(n_x3), edge_step(gra, x3, 4, gra.xn_ready, s3, mout, 3, 1, []), None),
            ])

        @block.vector
        def _(dve):
            V = nc.vector
            V.memset(w_f[:, :], 0.0).then_inc(w_zeroed, 1)
            V.memset(src_f[:, EP // 128:], 0.0).then_inc(spare_set, 1)
            V.memset(dst_f[:, EP // 128:], 0.0).then_inc(spare_set, 1)
            V.memset(dout[:, :, :, :], 0.0).then_inc(tables_f, 1)
            V.memset(d1_row[:, :, :], 0.0).then_inc(tables_f, 1)
            dve.wait_ge(lists_in, 64)
            V.tensor_copy(list_f[:, :, :], list_i[:, :, :]).then_inc(lists_float, 1)
            dve.wait_ge(loads, 16 * n_const)
            dve.wait_ge(tables_f, 2)
            V.tensor_copy(d1_row[:, :, 0:D], l1b[:, :].rearrange("p (a f) -> p a f", a=1).to_broadcast([128, 8, D])).then_inc(d1_row_ready, 1)
            dve.wait_ge(ready, 13)
            V.tensor_copy(dummy_f[:, :], dummy_i[:, :]).then_inc(tables_f, 1)
            dve.wait_ge(wT_psum, 1)
            V.tensor_copy(l1wT[:, :], bank[0][:, 0:128]).then_inc(wT_out, 1)
            dve.wait_ge(tables, 64)
            V.tensor_tensor(dev[:, :], dst_f[:, 0:EP // 128], even_i[:, :], ALU.subtract).then_inc(tables_f, 1)
            dve.wait_ge(tables_f, 4)
            V.tensor_reduce(lag_col[:, :], dev[:, :], AX.X, ALU.min).then_inc(lag_ready, 1)
            dve.wait_ge(lag_psum, 1)
            V.tensor_reduce(lag_min[:, :], bank[7][0:1, 0:128], AX.X, ALU.min).then_inc(tables_f, 1)
            dve.wait_ge(tables_f, 5)
            V.tensor_scalar(ascends[:, :], lag_min[:, :], -1024.0 * WINDOW, None, ALU.is_ge).then_inc(flag_ready, 1)

            def cols(t, n):
                return t[:, bass.ds(n * 4, 4)]

            def copy_cols(to, of):
                return V.tensor_scalar(to, of, 1.0, None, ALU.mult)

            def set_gidx(e, n, slot, tabs):
                for j, tab in enumerate(tabs):
                    ins = V.tensor_scalar(gidx[:, slot, 4 * j:4 * j + 4], cols(tab, n), float(N - 1), None, ALU.min)
                ins.then_inc(e.gidx_ready, 1)

            def set_next_gidx(e, new, tabs):
                wait_past(dve, e.gathered[1 - new.slot()], 64 * len(tabs) * (new.use() + new.slot()))
                set_gidx(e, new.n + 1, 1 - new.slot(), tabs)

            def row_stats(steps, count, rows_of, st, mean_var, between=None):
                for s in range(count):
                    steps.inc(V.bn_stats(st[:, s, :], rows_of(s)))
                steps.wait()
                between()
                for s in range(count):
                    ins = V.bn_aggr(mean_var[:, s, :], st[:, s, :])
                return ins

            def scale_and_bias(e, steps, t, count):
                dve.wait_ge(e.sd_ready, t.n + 1)
                steps.inc(V.reciprocal(rstd[:, t.slot(), 0:count], sd[:, t.slot(), 0:count]))
                steps.wait()
                V.scalar_tensor_tensor(out=nmr[:, t.slot(), 0:count], in0=mv[:, t.slot(), 0:count, 0], scalar=-1.0,
                                       in1=rstd[:, t.slot(), 0:count], op0=ALU.mult, op1=ALU.mult).then_inc(e.norm_ready, 1)

            def equalities(t, batch):
                for s in range(4):
                    lo = 256 * (s // 2) if batch == 256 else 0
                    ins = V.tensor_scalar(eq[:, t.slot(), s, 0:batch].rearrange("q (b k p) -> q b k p", k=2, p=128),
                                          idx_row[:, t.slot(), lo:lo + batch].rearrange("q (b p k) -> q b k p", k=2, p=128),
                                          key[:, t.slot(), s:s + 1], None, ALU.is_equal)
                return ins

            def leaders(steps, t, batch):
                for s in range(4):
                    lo = 256 * (s // 2) if batch == 256 else 0
                    steps.inc(V.scalar_tensor_tensor(out=junk[:, s, 0:batch], in0=idx_row[:, t.slot(), lo:lo + batch],
                                                     scalar=key[:, t.slot(), s:s + 1], in1=rank[:, s, lo:lo + batch],
                                                     op0=ALU.is_equal, op1=ALU.mult, accum_out=cnt[:, s:s + 1]))
                steps.inc(V.tensor_tensor(off[:, :], dummy_f[:, :], key[:, t.slot(), :], ALU.subtract))
                steps.wait()
                steps.inc(V.scalar_tensor_tensor(out=off2[:, :], in0=cnt[:, :], scalar=LATER, in1=off[:, :], op0=ALU.is_ge, op1=ALU.mult))
                steps.wait()
                return V.tensor_tensor(sidx[:, t.slot(), :], off2[:, :], key[:, t.slot(), :], ALU.add)

            steps = Steps(dve, mlp.dve, 8 + 1)
            lead = Steps(dve, mlp.dve_lead, 1 + 6)
            set_gidx(mlp, 0, 0, (src_f, dst_f))

            def mlp_step(at):
                new, t = at(0), at(2)
                if new:
                    steps.begin(new)
                    set_next_gidx(mlp, new, (src_f, dst_f))
                    dve.wait_ge(mlp.gathered[new.slot()], 128 * (new.use() + 1))
                    row_stats(steps, 8, lambda s: rows[:, new.slot(), s, :], stats, mv[:, new.slot(), :, :],
                              lambda: t and lead_key(t)).then_inc(mlp.var_ready, 1)
                elif t:
                    lead_key(t)
                if t:
                    dve.wait_ge(mlp.row_loaded[t.slot()], 16 * (t.use() + 1))
                    wait_past(dve, mlp.summed, t.n - 1)
                    lead.wait()
                    equalities(t, 256).then_inc(mlp.eq_ready, 1)
                if new:
                    scale_and_bias(mlp, steps, new, 8)
                    steps.end()
                if t:
                    wait_past(dve, mlp.scattered, 64 * (t.n - 1))
                    leaders(lead, t, 256).then_inc(mlp.sidx_ready, 1)
                    dve.wait_ge(mlp.sidx_ready, t.n + 1)
                    dve.sem_inc(mlp.row_read, 1)
                    lead.end()
                    dve.wait_ge(msg_psum, t.n + 1)
                    V.tensor_tensor(msg[:, :, :], by4(bank[5][:, :]), row4(b2r), ALU.add).then_inc(msg_out, 1)

            def lead_key(t):
                lead.begin(t)
                lead.inc(copy_cols(key[:, t.slot(), :], cols(src_f, t.n)))

            run(dve, [Part(EDGE_TURNS, 2, mlp_step)])

            def sums_landed(e, then):
                def prepare():
                    dve.wait_ge(e.scattered, 64 * EDGE_TURNS)
                    set_gidx(then, 0, 0, (src_f,))
                return prepare

            def wag_step(at):
                new, old = at(0), at(1)
                if new:
                    wsteps.begin(new)
                    set_next_gidx(wag, new, (src_f,))
                if old:
                    wlead.begin(old)
                    wait_past(dve, wag.scattered, 64 * (old.n - 1))
                    leaders(wlead, old, 512).then_inc(wag.sidx_ready, 1)
                    wlead.inc(V.tensor_scalar(dout[:, old.slot(), :, D], cnt[:, :], 1.0, None, ALU.add))
                    dve.wait_ge(wag.sidx_ready, old.n + 1)
                    copy_cols(cols(leader, old.n), sidx[:, old.slot(), :]).then_inc(wag.row_read, 1)
                    wlead.end()
                if new:
                    dve.wait_ge(wag.gathered[new.slot()], 64 * (new.use() + 1))
                    row_stats(wsteps, 4, lambda s: rows[:, new.slot(), s, :], stats, mv[:, new.slot(), :, :],
                              lambda: wsteps.inc(copy_cols(key[:, new.slot(), :], cols(dst_f, new.n)))).then_inc(wag.var_ready, 1)
                if old:
                    wait_past(dve, aggT_psum, old.n)
                    dve.wait_ge(wag.xn_ready, old.n + 1)
                    V.tensor_tensor(xw[:, :, :], xn[:, 0:4, :], each4(w_f, old.n), ALU.mult).then_inc(xw_ready, 1)
                if new:
                    dve.wait_ge(wag.row_loaded[new.slot()], 16 * (new.use() + 1))
                    wait_past(dve, wag.summed, new.n - 1)
                    wsteps.wait()
                    equalities(new, 512).then_inc(wag.eq_ready, 1)
                    scale_and_bias(wag, wsteps, new, 4)
                    wsteps.end()

            wsteps = Steps(dve, wag.dve, 4 + 1 + 1)
            wlead = Steps(dve, wag.dve_lead, 6 + 1)

            xsteps = Steps(dve, n_x2.dve, 4)
            xsteps2 = Steps(dve, x2_norm_steps, 3)

            def x2_step(at):
                new, old = at(0), at(1)
                if new:
                    s, s4 = new.slot(), new.slot(4)
                    xsteps.begin(new)
                    dve.wait_ge(node_loaded[s4], n_x2.loaded(new))
                    wait_past(dve, node_stored[s4], n_x2.slot_stored(new))
                    V.tensor_tensor(by4(nt[:, s4, :]), by4(na[:, s4, :]), by4(nb[:, s4, :])[:, :, 0:D], ALU.add)\
                        .then_inc(x2_ready, 1)
                    dve.wait_ge(x2_ready, new.n + 1)
                    row_stats(xsteps, 4, lambda k: nt[:, s4, 128 * k:128 * k + 128], nstats, nmv[:, s, :, :],
                              lambda: V.tensor_copy(degree[:, s, :], by4(nb[:, s4, :])[:, :, D])).then_inc(n_x2.inputs_read, 1)
                    xsteps.end()
                if old:
                    s = old.slot()
                    xsteps2.begin(old)
                    dve.wait_ge(nsd_ready, old.n + 1)
                    xsteps2.inc(V.reciprocal(nrsd[:, s, :], nsd[:, s, :]))
                    xsteps2.wait()
                    xsteps2.inc(V.tensor_tensor(nrstd[:, s, :], nrsd[:, s, 0:4], nrsd[:, s, 4:8], ALU.mult))
                    xsteps2.inc(copy_cols(cols(dinv, old.n), nrsd[:, s, 4:8]))
                    xsteps2.wait()
                    V.scalar_tensor_tensor(out=nnmr[:, s, :], in0=nmv[:, s, :, 0], scalar=-1.0, in1=nrstd[:, s, :],
                                           op0=ALU.mult, op1=ALU.mult).then_inc(x2_norm, 1)
                    xsteps2.end()

            def plain_edges(e, norm):
                psteps = Steps(dve, e.dve, 1 + (5 if norm else 0))

                def step(at):
                    t, old = at(0), at(1)
                    if old:
                        wait_past(dve, e.scattered, 64 * (old.n - 1))
                        copy_cols(sidx[:, old.slot(), :], cols(leader, old.n)).then_inc(e.sidx_ready, 1)
                    if not t:
                        return

                    def keys():
                        psteps.inc(copy_cols(key[:, t.slot(), :], cols(dst_f, t.n)))
                    psteps.begin(t)
                    set_next_gidx(e, t, (src_f,))
                    if norm:
                        dve.wait_ge(e.gathered[t.slot()], 64 * (t.use() + 1))
                        row_stats(psteps, 4, lambda s: rows[:, t.slot(), s, :], stats, mv[:, t.slot(), :, :], keys).then_inc(e.var_ready, 1)
                    else:
                        keys()
                    dve.wait_ge(e.row_loaded[t.slot()], 16 * (t.use() + 1))
                    wait_past(dve, e.summed, t.n - 1)
                    psteps.wait()
                    equalities(t, 512).then_inc(e.eq_ready, 1)
                    if norm:
                        scale_and_bias(e, psteps, t, 4)
                    dve.wait_ge(e.eq_ready, t.n + 1)
                    dve.sem_inc(e.row_read, 1)
                    psteps.end()
                return step, 1

            def gcn_step(at):
                new, mid, old = at(0), at(1), at(2)
                if new:
                    s4 = new.slot(4)
                    dve.wait_ge(node_loaded[s4], n_gcn.loaded(new))
                    wait_past(dve, n_gcn.turned, new.n - 3)
                    V.tensor_tensor(by4(nt[:, s4, :]), by4(na[:, s4, :]), each4(dinv, new.n), ALU.mult)\
                        .then_inc(n_gcn.inputs_read, 1)
                if old:
                    s4 = old.slot(4)
                    dve.wait_ge(n_gcn.product, old.n + 1)
                    wait_past(dve, node_stored[s4], n_gcn.slot_stored(old))
                    V.tensor_tensor(by4(no[:, s4, :]), by4(bank[5][:, :]), each4(dinv, old.n), ALU.mult).then_inc(n_gcn.result, 1)
                if mid:
                    for c in (2, 3):
                        dve.wait_ge(ghid_psum, 4 * mid.n + c + 1)
                        V.tensor_scalar(nhid[:, c, :], bank[1 + c][:, :], gb1[:, c:c + 1], 0.0, ALU.add, ALU.max)\
                            .then_inc(ghid_dve, 1)

            x3steps = Steps(dve, n_x3.dve, 2)

            def x3_step(at):
                t, s4 = at(0), at(0).slot(4)
                x3steps.begin(t)
                dve.wait_ge(node_loaded[s4], n_x3.loaded(t))
                x3steps.inc(V.tensor_tensor(by4(ntmp[:, 0, :]), by4(nb[:, s4, 0:512]), each4(dinv, t.n), ALU.mult))
                x3steps.wait()
                x3steps.inc(V.tensor_tensor(by4(ntmp[:, 1, :]), by4(ntmp[:, 0, :]), row4(gb2), ALU.add))
                x3steps.wait()
                wait_past(dve, node_stored[s4], n_x3.slot_stored(t))
                V.scalar_tensor_tensor(out=no[:, s4, :], in0=ntmp[:, 1, :], scalar=0.0, in1=na[:, s4, :],
                                       op0=ALU.max, op1=ALU.add).then_inc(n_x3.result, 1)
                x3steps.end()

            osteps = Steps(dve, n_out.dve, 1)

            def out_step(at):
                t = at(1)
                if t:
                    s4 = t.slot(4)
                    osteps.begin(t)
                    dve.wait_ge(n_out.product, t.n + 1)
                    osteps.inc(V.tensor_tensor(by4(ntmp[:, 0, :]), by4(bank[1][:, :]), row4(l3b), ALU.add))
                    osteps.wait()
                    wait_past(dve, node_stored[s4], n_out.slot_stored(t))
                    V.scalar_tensor_tensor(out=no[:, s4, :], in0=ntmp[:, 0, :], scalar=0.0, in1=na[:, s4, :],
                                           op0=ALU.max, op1=ALU.add).then_inc(n_out.result, 1)
                    osteps.end()

            passes(dve, [
                (sums_landed(mlp, wag), (wag_step, 1), (lambda together: x2_step, 1)),
                (sums_landed(wag, gc1), plain_edges(gc1, False), (lambda together: gcn_step, 2)),
                (sums_landed(gc1, gc2), plain_edges(gc2, False), (lambda together: x3_step, 0)),
                (sums_landed(gc2, gra), plain_edges(gra, True), (lambda together: out_step, 1)),
            ])

        @block.scalar
        def _(act):
            S = nc.scalar
            act.wait_ge(loads, 16 * n_const)
            act.wait_ge(tables, 64)
            act.dma_start(x1[0:N, :].rearrange("(a r) f -> a (r f)", a=800), x.rearrange("(a r) f -> a (r f)", a=800)).then_inc(x1_set, 16)
            act.wait_ge(zero_ready, 2)
            act.dma_start(x1[N:NP, :].rearrange("(p r) f -> p (r f)", r=4), zero[0:(NP - N) // 4, 0:4 * D]).then_inc(x1_set, 16)

            def root(e, t, count):
                act.wait_ge(e.var_ready, t.n + 1)
                S.activation(sd[:, t.slot(), 0:count], mv[:, t.slot(), 0:count, 1], ACT.Sqrt, bias=eps_c[:, :]).then_inc(e.sd_ready, 1)

            def normalise(e, t, count, func):
                act.wait_ge(e.norm_ready, t.n + 1)
                for s in range(count):
                    ins = S.activation(xn[:, s, :], rows[:, t.slot(), s, :], func, bias=nmr[:, t.slot(), s:s + 1],
                                       scale=rstd[:, t.slot(), s:s + 1])
                ins.then_inc(e.xn_ready, 1)

            def sums_out(e, t, of, to):
                act.wait_ge(e.summed, t.n + 1)
                wait_past(act, e.scattered, 64 * (t.n - 1))
                S.activation(to[:, t.slot(), :, 0:D], by4(of[:, :]), ACT.Copy).then_inc(e.out_ready, 1)

            def mlp_step(at):
                if at(0):
                    root(mlp, at(0), 8)
                if at(2):
                    for c in range(2):
                        act.wait_ge(hid_psum, 2 * at(2).n + c + 1)
                        S.activation(ehid[:, c, :], bank[3 + c][:, :], ACT.Relu, bias=b1c[:, c:c + 1]).then_inc(hid_out, 1)
                if at(1):
                    for j, (to, of, func) in enumerate(((hTs, bank[0], ACT.Relu), (hTd, bank[1], ACT.Relu), (eT, bank[2], ACT.Copy))):
                        act.wait_ge(turned, 3 * at(1).n + j + 1)
                        p = 64 if j == 2 else 128
                        S.activation(to[:, :], of[0:p, :], func).then_inc(turned_out, 1)
                if at(3):
                    sums_out(mlp, at(3), bank[6], mout)
                if at(0):
                    normalise(mlp, at(0), 8, ACT.Identity)

            run(act, [Part(EDGE_TURNS, 3, mlp_step)])

            def wag_step(at):
                if at(0):
                    root(wag, at(0), 4)
                if at(1):
                    act.wait_ge(aggT_psum, at(1).n + 1)
                    S.activation(hTs[:, :], bank[0][:, :], ACT.Copy).then_inc(aggT_out, 1)
                if at(0):
                    wait_past(act, xw_ready, at(0).n)
                    normalise(wag, at(0), 4, ACT.Relu)
                if at(1):
                    sums_out(wag, at(1), bank[1], dout)

            def h2_step(at):
                new, old = at(0), at(1)
                if new:
                    s = new.slot()
                    act.wait_ge(n_x2.inputs_read, new.n + 1)
                    S.activation(nsd[:, s, 0:4], nmv[:, s, :, 1], ACT.Sqrt, bias=eps_c[:, :])
                    S.activation(nsd[:, s, 4:8], degree[:, s, :], ACT.Sqrt, bias=1.0).then_inc(nsd_ready, 1)
                if old:
                    s, s4 = old.slot(), old.slot(4)
                    act.wait_ge(x2_norm, old.n + 1)
                    wait_past(act, node_stored[s4], n_x2.slot_stored(old))
                    for k in range(4):
                        f = slice(128 * k, 128 * k + 128)
                        ins = S.activation(no[:, s4, f], nt[:, s4, f], ACT.Relu, bias=nnmr[:, s, k:k + 1], scale=nrstd[:, s, k:k + 1])
                    ins.then_inc(n_x2.result, 1)

            def plain_out(e):
                return lambda at: at(0) and sums_out(e, at(0), bank[6 + at(0).slot()], mout)

            def gcn_step(at):
                t = at(0)
                act.wait_ge(n_gcn.turned, t.n + 1)
                S.activation(nT[:, 0, :], bank[0][:, :], ACT.Copy).then_inc(n_gcn.turned_out, 1)
                for c in range(2):
                    act.wait_ge(ghid_psum, 4 * t.n + c + 1)
                    S.activation(nhid[:, c, :], bank[1 + c][:, :], ACT.Relu, bias=gb1[:, c:c + 1]).then_inc(ghid_act, 1)

            def gra_step(at):
                if at(0):
                    root(gra, at(0), 4)
                    wait_past(act, gra.summed, at(0).n)
                    normalise(gra, at(0), 4, ACT.Relu)
                if at(1):
                    sums_out(gra, at(1), bank[6], mout)

            def out_step(at):
                t = at(0)
                act.wait_ge(n_out.turned, t.n + 1)
                S.activation(nT[:, t.slot(), :], bank[0][:, :], ACT.Copy).then_inc(n_out.turned_out, 1)

            def nothing():
                pass

            passes(act, [
                (nothing, (wag_step, 1), (lambda together: h2_step, 1)),
                (nothing, (plain_out(gc1), 0), (lambda together: gcn_step, 0)),
                (nothing, (plain_out(gc2), 0), None),
                (nothing, (gra_step, 1), (lambda together: out_step, 0)),
            ])

        @block.tensor
        def _(pe):
            T = nc.tensor
            pe.wait_ge(ready, 13)
            pe.wait_ge(loads, 16 * n_const)
            T.transpose(bank[0][:, 0:128], l1w[:, :], ident[:, :]).then_inc(wT_psum, 1)
            pe.wait_ge(lag_ready, 1)
            T.transpose(bank[7][0:1, 0:128], lag_col[:, :], ident[:, :]).then_inc(lag_psum, 1)
            pe.wait_ge(wT_out, 1)

            def turn_rows(to, of):
                for s in range(4):
                    ins = T.transpose(to[:, 128 * s:128 * s + 128], of(s), ident[:, :])
                return ins

            def batch_sums(to, of, slot, batch):
                per = batch // 128
                for s2 in range(4):
                    c = s2 % per
                    for k in range(per):
                        s = s2 - c + k
                        ins = T.matmul(to[:, 128 * s2:128 * s2 + 128], eq[:, slot, s, 128 * c:128 * c + 128],
                                       of(s), start=(k == 0), stop=(k == per - 1))
                return ins

            def mlp_step(at):
                t1, t2, t3 = at(1), at(2), at(3)
                if t2:
                    pe.wait_ge(turned_out, 3 * t2.n + 3)
                    wait_past(pe, hid_out, 2 * t2.n)
                    for c in range(2):
                        f = slice(128 * c, 128 * c + 128)
                        T.matmul(bank[3 + c][:, :], w1s[:, f], hTs[:, :], start=True, stop=False)
                        T.matmul(bank[3 + c][:, :], w1d[:, f], hTd[:, :], start=False, stop=False)
                        T.matmul(bank[3 + c][:, :], w1e[:, f], eT[:, :], start=False, stop=True).then_inc(hid_psum, 1)
                if t1:
                    pe.wait_ge(ea_loaded[t1.slot()], 16 * (t1.use() + (2 if last_turn(t1) else 1)))
                    pe.wait_ge(mlp.xn_ready, t1.n + 1)
                    wait_past(pe, turned_out, 3 * t1.n)
                    turn_rows(bank[0], lambda s: xn[:, s, :]).then_inc(turned, 1)
                    turn_rows(bank[1], lambda s: xn[:, 4 + s, :]).then_inc(turned, 1)
                    for s in range(4):
                        ins = T.transpose(bank[2][0:64, 128 * s:128 * s + 128], eav[:, t1.slot(), s, :], ident[:, :])
                    ins.then_inc(turned, 1)
                if t3:
                    pe.wait_ge(msg_out, t3.n + 1)
                    pe.wait_ge(mlp.eq_ready, t3.n + 1)
                    wait_past(pe, mlp.out_ready, t3.n)
                    batch_sums(bank[6], lambda s: msg[:, s, :], t3.slot(), 256).then_inc(mlp.summed, 1)
                if t2:
                    pe.wait_ge(hid_out, 2 * t2.n + 2)
                    wait_past(pe, msg_out, t2.n)
                    for s in range(4):
                        f = slice(128 * s, 128 * s + 128)
                        for c in range(2):
                            ins = T.matmul(bank[5][:, f], ehid[:, c, f], w2c[:, c, :], start=(c == 0), stop=(c == 1))
                    ins.then_inc(msg_psum, 1)

            run(pe, [Part(EDGE_TURNS, 3, mlp_step)])

            def wag_step(at):
                t = at(0)
                if t:
                    pe.wait_ge(xw_ready, t.n + 1)
                    pe.wait_ge(wag.eq_ready, t.n + 1)
                    wait_past(pe, aggT_out, t.n)
                    for s in range(4):
                        ins = T.matmul(bank[0][:, :], xw[:, s, :], eq[:, t.slot(), s, :], start=(s == 0), stop=(s == 3))
                    ins.then_inc(aggT_psum, 1)
                    pe.wait_ge(aggT_out, t.n + 1)
                    wait_past(pe, wag.out_ready, t.n)
                    for s in range(4):
                        f = slice(128 * s, 128 * s + 128)
                        ins = T.matmul(bank[1][:, f], hTs[:, f], l1wT[:, :], start=True, stop=True)
                    ins.then_inc(wag.summed, 1)

            def plain_sums(e):
                def step(at):
                    t = at(0)
                    if t:
                        pe.wait_ge(e.gathered[t.slot()], 64 * (t.use() + 1))
                        pe.wait_ge(e.eq_ready, t.n + 1)
                        wait_past(pe, e.out_ready, t.n - 1)
                        batch_sums(bank[6 + t.slot()], lambda s: rows[:, t.slot(), s, :], t.slot(), 512).then_inc(e.summed, 1)
                return step, 0

            def gcn_step(at):
                new, old = at(0), at(1)
                if new:
                    pe.wait_ge(n_gcn.inputs_read, new.n + 1)
                    wait_past(pe, n_gcn.turned_out, new.n)
                    turn_rows(bank[0], lambda s: nt[:, new.slot(4), 128 * s:128 * s + 128]).then_inc(n_gcn.turned, 1)
                if old:
                    pe.wait_ge(ghid_act, 2 * old.n + 2)
                    pe.wait_ge(ghid_dve, 2 * old.n + 2)
                    wait_past(pe, n_gcn.result, old.n)
                    for s in range(4):
                        f = slice(128 * s, 128 * s + 128)
                        for c in range(4):
                            ins = T.matmul(bank[5][:, f], nhid[:, c, f], gw2[:, c, :], start=(c == 0), stop=(c == 3))
                    ins.then_inc(n_gcn.product, 1)
                if new:
                    pe.wait_ge(n_gcn.turned_out, new.n + 1)
                    for c in range(4):
                        T.matmul(bank[1 + c][:, :], gw1[:, 128 * c:128 * c + 128], nT[:, 0, :], start=True, stop=True)\
                            .then_inc(ghid_psum, 1)

            def gra_step(at):
                t = at(0)
                if t:
                    pe.wait_ge(gra.xn_ready, t.n + 1)
                    pe.wait_ge(gra.eq_ready, t.n + 1)
                    wait_past(pe, gra.out_ready, t.n)
                    batch_sums(bank[6], lambda s: xn[:, s, :], t.slot(), 512).then_inc(gra.summed, 1)

            def out_step(at):
                new, old = at(0), at(1)
                if new:
                    pe.wait_ge(node_loaded[new.slot(4)], n_out.loaded(new))
                    wait_past(pe, n_out.turned_out, new.n)
                    turn_rows(bank[0], lambda s: nb[:, new.slot(4), 128 * s:128 * s + 128]).then_inc(n_out.turned, 1)
                if old:
                    pe.wait_ge(n_out.turned_out, old.n + 1)
                    wait_past(pe, n_out.result, old.n)
                    for s in range(4):
                        f = slice(128 * s, 128 * s + 128)
                        ins = T.matmul(bank[1][:, f], nT[:, old.slot(), f], l3w[:, :], start=True, stop=True)
                    ins.then_inc(n_out.product, 1)

            def nothing():
                pass

            passes(pe, [
                (nothing, (wag_step, 0), None),
                (nothing, plain_sums(gc1), (lambda together: gcn_step, 1)),
                (nothing, plain_sums(gc2), None),
                (nothing, (gra_step, 0), (lambda together: out_step, 1)),
            ])


_INS = ["x", "src", "dst", "edge_attr_64", "edge_weight", "L0_gnn_W1", "L0_gnn_b1", "L0_gnn_W2", "L0_gnn_b2", "L1_gnn_W",
        "L1_gnn_b", "L2_gnn_W1", "L2_gnn_b1", "L2_gnn_W2", "L2_gnn_b2", "L3_gnn_W", "L3_gnn_b"]


def kernel(**inputs):
    import numpy as _np
    import concourse.bacc as _bacc
    from concourse import mybir as _mybir
    from concourse.bass_utils import run_bass_kernel_spmd as _run

    nc = _bacc.Bacc("TRN2", target_bir_lowering=False, num_devices=1)
    arrays, args = {}, []
    for name in _INS:
        a = _np.ascontiguousarray(inputs[name])
        arrays[f"in_{name}_dram"] = a
        args.append(nc.dram_tensor(f"in_{name}_dram", a.shape, _mybir.dt.from_np(a.dtype), kind="ExternalInput").ap())
    args.append(nc.dram_tensor("out_0_dram", (N, D), _mybir.dt.float32, kind="ExternalOutput").ap())
    build(nc, *args)
    r = _run(nc, [arrays], core_ids=[0])
    return r.results[0]["out_0_dram"]
```

```python
import concourse.bass as bass
from concourse import mybir
from contextlib import ExitStack

F32 = mybir.dt.float32
F32R = mybir.dt.float32r
I32 = mybir.dt.int32
ALU = mybir.AluOpType
ACT = mybir.ActivationFunctionType
AX = mybir.AxisListType

D = 128
N = 100000
E = 50000
NODE_TURNS = -(-N // 512)
NP = NODE_TURNS * 512
EDGE_TURNS = -(-E // 512)
EP = EDGE_TURNS * 512
DUMMY = NP
NR = NP + 512
PAD_INDEX = N
DW = D + 4
LATER = 1024.0
EPS = 1e-5
BLOCK = 16
WINDOW = 384
TILES = WINDOW // 128
BLOCKS = WINDOW // BLOCK
HALF = NODE_TURNS // 2
LIST = EP // 112
assert NODE_TURNS == 2 * EDGE_TURNS and NODE_TURNS % 4 == 0 and NP == 1024 * EDGE_TURNS
assert LIST % BLOCK == 0 and HALF <= 128
assert E % 2 == 0 and PAD_INDEX < NP


class Turn:

    def __init__(self, i, const, stride=0):
        self.i, self.const, self.stride = i, const, stride
        self.n = const if i is None else i * stride + const

    def slot(self, d=2):
        assert self.stride % d == 0
        return self.const % d

    def use(self, d=2):
        return self.const // d if self.i is None else i_times(self.i, self.stride // d) + self.const // d

    def first(self):
        return self.i is None and self.const == 0


def i_times(i, k):
    return i if k == 1 else i * k


class Part:

    def __init__(self, count, lag, step):
        self.count, self.lag, self.step = count, lag, step


def run(eng, part, oldest=4):
    unroll = 4 if part.count == NODE_TURNS else 2
    first = part.lag + oldest
    first += (part.count - first) % unroll

    def turn(const, i=None):
        def at(k):
            if i is None and not 0 <= const - k < part.count:
                return None
            return Turn(i, const - k, 0 if i is None else unroll)
        part.step(at)

    for c in range(first):
        turn(c)
    with eng.Fori(0, (part.count - first) // unroll) as i:
        for u in range(unroll):
            turn(first + u, i)
    for c in range(part.count, part.count + part.lag):
        turn(c)


def wait_past(eng, sem, value):
    if not isinstance(value, int) or value > 0:
        eng.wait_ge(sem, value)


class Steps:

    def __init__(self, eng, sem, per_turn):
        self.eng, self.sem, self.per_turn, self.turn, self.done = eng, sem, per_turn, None, 0

    def begin(self, turn):
        self.turn, self.done = turn, 0

    def inc(self, instruction):
        self.done += 1
        instruction.then_inc(self.sem, 1)

    def wait(self):
        self.eng.wait_ge(self.sem, self.turn.n * self.per_turn + self.done)

    def end(self):
        assert self.done == self.per_turn, (self.done, self.per_turn)


def build(nc, x, src, dst, ea, ew, m1_w1, m1_b1, m1_w2, m1_b2, l1_w, l1_b, g_w1, g_b1, g_w2, g_b2, l3_w, l3_b, out):
    ctx = ExitStack()

    def sb(name, shape, dt=F32):
        return ctx.enter_context(nc.sbuf_tensor(name, shape, dt))

    def sem(name):
        return ctx.enter_context(nc.semaphore(name))

    def dram(name, shape, dt=F32):
        return nc.dram_tensor(name, shape, dt, kind="Internal").ap()

    with ctx:
        src_pad = dram("src_pad", [EP])
        dst_pad = dram("dst_pad", [EP])
        blocks = dram("blocks", [EP // BLOCK + BLOCKS, 3, BLOCK])
        x1 = dram("x1", [NR, D])
        d1 = dram("d1", [NR, DW])
        x2 = dram("x2", [NP, D])
        h2 = dram("h2", [NP, D])
        s2 = dram("s2", [NR, D])
        z2 = dram("z2", [NP, D])
        t2 = dram("t2", [NR, D])
        x3 = dram("x3", [NP, D])
        s3 = dram("s3", [NR, D])

        ident = sb("ident", [128, 128])
        rank = sb("rank", [128, 4, 512])
        dummy_i = sb("dummy_i", [128, 4], I32)
        dummy_f = sb("dummy_f", [128, 4])
        lag_col = sb("lag_col", [128, 1])
        lag_min = sb("lag_min", [1, 1])
        ascends = sb("ascends", [1, 1], I32)
        zero = sb("zero", [128, 8 * D])
        d1_row = sb("d1_row", [128, 8, DW])
        eps_c = sb("eps_c", [128, 1])
        list_i = sb("list_i", [112, 3, LIST], I32)
        list_f = sb("list_f", [112, 3, LIST])
        list_w = sb("list_w", [112, LIST])
        last_blocks = sb("last_blocks", [BLOCKS, 3, BLOCK])
        step_up = sb("step_up", [112, LIST])
        up_col = sb("up_col", [128, 1])
        first_node_i = sb("first_node_i", [112, NODE_TURNS + 1], I32)
        first_node = sb("first_node", [112, NODE_TURNS + 1])
        below = sb("below", [112, NODE_TURNS + 1])
        ones = sb("ones", [128, 128])
        start = sb("start", [HALF, 2, 2])
        start_i = sb("start_i", [HALF, 2], I32)
        block_i = sb("block_i", [HALF, 2], I32)
        block_f = sb("block_f", [HALF, 2])
        over = sb("over", [HALF, 2])
        over_col = sb("over_col", [128, 1])
        block_no_i = sb("block_no_i", [HALF, BLOCKS], I32)
        block_no = sb("block_no", [HALF, BLOCKS])
        window_block = sb("window_block", [HALF, 2, BLOCKS], I32)
        base_i = sb("base_i", [128, NODE_TURNS, TILES], I32)
        base_f = sb("base_f", [128, NODE_TURNS, TILES])
        node_no_i = sb("node_no_i", [128, 512], I32)
        node_no = sb("node_no", [128, 512])
        win_src = sb("win_src", [128, NODE_TURNS + 3, TILES])
        win_dst = sb("win_dst", [128, NODE_TURNS, TILES])
        win_key = sb("win_key", [128, NODE_TURNS, TILES])
        win_w = sb("win_w", [128, NODE_TURNS, TILES])
        w1s, w1d = sb("w1s", [128, 256]), sb("w1d", [128, 256])
        w1e = sb("w1e", [64, 256])
        b1c = sb("b1c", [128, 2])
        w2c = sb("w2c", [128, 2, 128])
        l1w = sb("l1w", [128, 128])
        l1wT = sb("l1wT", [128, 128])
        l1b = sb("l1b", [128, 128])
        gw1 = sb("gw1", [128, 512])
        gb1 = sb("gb1", [128, 4])
        gw2 = sb("gw2", [128, 4, 128])
        gb2 = sb("gb2", [128, 128])
        l3w = sb("l3w", [128, 128])
        l3b = sb("l3b", [128, 128])
        bias_rows = sb("bias_rows", [128, 3, 128])
        bias_high = sb("bias_high", [128, 3, 128])
        bias_split = sb("bias_split", [128, 3, 128])
        src_f = sb("src_f", [128, EP // 128 + 4])
        dst_f = sb("dst_f", [128, EP // 128 + 4])
        w_f = sb("w_f", [128, EP // 128])
        leader = sb("leader", [128, EP // 128], I32)
        dinv = sb("dinv", [128, 4 * NODE_TURNS])

        rows = sb("rows", [128, 2, 8, 128])
        xn = sb("xn", [128, 8, 128])
        xw = sb("xw", [128, 2, 4, 128])
        eav = sb("eav", [128, 2, 4, 64])
        high = sb("high", [128, 2, 4, 128])
        low = sb("low", [128, 2, 4, 128])
        idx_row = sb("idx_row", [128, 2, 512])
        key = sb("key", [128, 2, 4])
        gidx = sb("gidx", [128, 2, 8], I32)
        wgidx = sb("wgidx", [128, 4, TILES], I32)
        sidx = sb("sidx", [128, 2, 4], I32)
        eq = sb("eq", [128, 2, 4, 512])
        junk = sb("junk", [128, 4, 512])
        stats = sb("stats", [128, 8, 6])
        mv = sb("mv", [128, 2, 8, 2])
        sd = sb("sd", [128, 2, 8])
        rstd = sb("rstd", [128, 2, 8])
        nmr = sb("nmr", [128, 2, 8])
        cnt = sb("cnt", [128, 4])
        off = sb("off", [128, 4])
        off2 = sb("off2", [128, 4])
        hTs, hTd = sb("hTs", [128, 512]), sb("hTd", [128, 512])
        eT = sb("eT", [64, 512])
        ehid = sb("ehid", [128, 2, 512])
        mout = sb("mout", [128, 2, 4, 128])
        dout = sb("dout", [128, 2, 4, DW])

        na = sb("na", [128, 4, 512])
        nb = sb("nb", [128, 4, 4 * DW])
        nt = sb("nt", [128, 4, 512])
        no = sb("no", [128, 4, 512])
        ntmp = sb("ntmp", [128, 2, 512])
        nT = sb("nT", [128, 2, 512])
        nhid = sb("nhid", [128, 4, 512])
        nstats = sb("nstats", [128, 4, 6])
        nmv = sb("nmv", [128, 2, 4, 2])
        nsd = sb("nsd", [128, 2, 8])
        nrsd = sb("nrsd", [128, 2, 8])
        nrstd = sb("nrstd", [128, 2, 4])
        nnmr = sb("nnmr", [128, 2, 4])
        dinv_x3 = sb("dinv_x3", [128, 4, 4])
        degree = sb("degree", [128, 2, 4])

        bank = [ctx.enter_context(nc.psum_tensor(f"bank{i}", [128, 512], F32)) for i in range(8)]

        zero_ready = sem("zero_set")
        d1_row_ready = sem("d1_row_set")
        ready = sem("constants_ready")
        loads = sem("constants_loaded")
        pad_ready = sem("pad_index_set")
        lists_in = sem("lists_in")
        lists_float = sem("lists_float")
        lists_out = sem("lists_out")
        spare_set = sem("spare_group_set")
        tables = sem("tables_loaded")
        x1_set = sem("x1_set")
        dummies_set = sem("dummy_rows_set")
        targets_set = sem("d1_and_s3_set")
        gates = sem("pool_gates")
        sp_gates = sem("sp_gates")
        tables_f = sem("tables_float")
        wT_psum = sem("l1_weight_transposed")
        wT_out = sem("l1_weight_copied")
        lag_ready = sem("dst_lag_ready")
        lag_psum = sem("dst_lag_transposed")
        flag_ready = sem("ascends_ready")

        class Edge:

            def __init__(self, tag, norm=True, lead=False):
                self.gidx_ready = sem(f"{tag}_gidx_ready")
                self.loaded = [sem(f"{tag}_loaded{u}") for u in range(4)]
                self.gathered = self.loaded[0:2]
                self.row_loaded = self.loaded[2:4]
                self.row_read = sem(f"{tag}_idx_row_read")
                self.eq_ready = sem(f"{tag}_eq_ready")
                self.sidx_ready = sem(f"{tag}_sidx_ready")
                self.summed = sem(f"{tag}_summed")
                self.out_ready = sem(f"{tag}_out_ready")
                self.scattered = sem(f"{tag}_scattered")
                self.dve = sem(f"{tag}_dve_steps")
                if lead:
                    self.dve_lead = sem(f"{tag}_dve_leader_steps")
                if norm:
                    self.var_ready = sem(f"{tag}_var_ready")
                    self.sd_ready = sem(f"{tag}_sd_ready")
                    self.norm_ready = sem(f"{tag}_norm_ready")
                    self.xn_ready = sem(f"{tag}_xn_ready")

        node_loaded = [sem(f"node_loaded{u}") for u in range(4)]
        node_stored = [sem(f"node_stored{u}") for u in range(4)]

        class Flow:

            def __init__(self, loads, stores, after):
                self.loads, self.stores = 16 * loads, 16 * stores
                self.loads_before = after.loads_before + after.loads * NODE_TURNS // 4 if after else 0
                self.stores_before = after.stores_before + after.stores * NODE_TURNS // 4 if after else 0
                self.stores_done = self.stores_before + self.stores * NODE_TURNS // 4

            def loaded(self, t):
                return self.loads_before + self.loads * (t.use(4) + 1)

            def slot_stored(self, t):
                return self.stores_before + self.stores * t.use(4)

        class Node(Flow):

            def __init__(self, tag, loads, stores, after, own):
                super().__init__(loads, stores, after)
                self.result = sem(f"{tag}_result")
                self.inputs_read = sem(f"{tag}_inputs_read") if "inputs" in own else self.result
                if "turn" in own:
                    self.turned = sem(f"{tag}_turned")
                    self.turned_out = sem(f"{tag}_turned_out")
                    self.product = sem(f"{tag}_product")
                if "dve" in own:
                    self.dve = sem(f"{tag}_dve_steps")

        mlp, wag, gc1, gc2, gra = Edge("mlp", lead=True), Edge("wag", lead=True), Edge("gc1", norm=False), Edge("gc2", norm=False), Edge("gra")
        n_x2 = Node("n_x2", 2, 3, None, ("inputs", "dve"))
        n_gcn = Node("n_gcn", 1, 2, n_x2, ("inputs", "turn"))
        n_x3 = Node("n_x3", 2, 1, n_gcn, ("dve",))
        n_out = Node("n_out", 2, 1, n_x3, ("turn", "dve"))


        class Windowed(Flow):

            def __init__(self, e, n, loads, stores, after):
                super().__init__(loads, stores, after)
                self.e, self.n = e, n
                self.gidx_ready, self.gathered = e.gidx_ready, e.loaded
                self.eq_ready, self.summed, self.sums_out = e.eq_ready, e.summed, e.out_ready
                self.result = n.result

        w_x2 = Windowed(wag, n_x2, 1, 2, None)
        w_gcn = Windowed(gc1, n_gcn, 1, 1, w_x2)
        w_x3 = Windowed(gc2, n_x3, 2, 1, w_gcn)
        w_out = Windowed(gra, n_out, 1, 1, w_x3)
        ea_loaded = [sem(f"ea_loaded{u}") for u in range(2)]
        turned = sem("mlp_turned")
        turned_out = sem("mlp_turned_out")
        hid_psum = sem("mlp_hidden")
        hid_out = sem("mlp_hidden_out")
        msg_psum = sem("mlp_messages")
        msg_high = sem("mlp_messages_high")
        msg_split = sem("mlp_messages_split")
        split_steps = sem("gcn_split_steps")
        split_ready = sem("gcn_rows_split")
        out_split = sem("out_rows_split")
        own_added = sem("x3_own_rows_added")
        gra_scale_steps = sem("gra_scale_steps")
        product = sem("window_product")
        bias_rows_zeroed = sem("bias_rows_zeroed")
        win_iotas = sem("window_iotas")
        below_steps = sem("edges_below_steps")
        window_lists_set = sem("window_lists_set")
        window_block_set = sem("window_blocks_set")
        counted = sem("edges_below_counted")
        counts_psum = sem("edges_below_summed")
        start_steps = sem("window_start_steps")
        blocks_out = sem("blocks_out")
        blocks_in = sem("window_blocks_gathered")
        win_psum = sem("window_tables_transposed")
        win_out = sem("window_tables_copied")
        xw_ready = sem("wag_weighted_rows")
        aggT_psum = sem("wag_sums_transposed")
        aggT_out = sem("wag_sums_copied")
        x2_ready = sem("x2_ready")
        x2_norm = sem("x2_norm_ready")
        x2_norm_steps = sem("x2_norm_steps")
        nsd_ready = sem("x2_sd_ready")
        ghid_psum = sem("gcn_hidden")
        ghid_act = sem("gcn_hidden_act")
        ghid_dve = sem("gcn_hidden_dve")

        ea_flat = ea.rearrange("e f -> (e f)")
        last_rows = N - (NODE_TURNS - 1) * 512
        full = (E // 256) * 256
        rest = (E - full) // 2
        n_const = 19

        def nodes(a, n, count=512):
            return a[bass.ds(n * 512, count), :].rearrange("(p k) f -> p (k f)", k=4)

        def by4(t):
            return t.rearrange("p (s f) -> p s f", s=4)

        def row4(t):
            return t[:, :].rearrange("p (a f) -> p a f", a=1).to_broadcast([128, 4, 128])

        def each4(t, n):
            return t[:, bass.ds(n * 4, 4)].rearrange("p (s a) -> p s a", a=1).to_broadcast([128, 4, 128])

        def last_turn(t):
            return t.i is None and t.n == EDGE_TURNS - 1

        def passes(eng, prepare, windowed, batched):
            eng.wait_ge(flag_ready, 1)
            flag = eng.value_load(ascends[0:1, 0:1], min_val=0, max_val=1)
            with eng.If(flag == 1):
                for before, part in windowed:
                    before()
                    if part:
                        run(eng, part)
            with eng.Else():
                prepare()
                for before, *parts in batched:
                    before()
                    for part in parts:
                        if part:
                            run(eng, part)

        def nothing():
            pass

        def rows4(t):
            return rows[:, :, :, :].rearrange("p u (v s) f -> p (u v) s f", s=4)[:, t.slot(4), :, :]

        def xn2(t):
            return xn[:, 4 * t.slot():4 * t.slot() + 4, :]

        def window_lists(buf):
            return buf[0:HALF, :, :].rearrange("g u f -> g (u f)")[:, 0:3 * WINDOW]

        def win(tab, t):
            return tab[:, bass.ds(t.n, 1), :].rearrange("p a s -> p (a s)")

        block = ctx.enter_context(nc.Block())

        @block.sync
        def _(sp):
            w = LIST
            sp.wait_ge(pad_ready, 3)
            for j, (of, lo) in enumerate(((src, 0), (dst, 0), (dst, 1))):
                whole = (E - lo) // w
                sp.dma_start(list_i[0:whole, j, :], of[lo:lo + whole * w].rearrange("(a b) -> a b", b=w)).then_inc(lists_in, 16)
                sp.dma_start(list_i[whole:whole + 1, j, 0:E - lo - whole * w], of[lo + whole * w:E].rearrange("(a b) -> a b", a=1)).then_inc(lists_in, 16)
            sp.dma_start(list_w[0:E // w, :], ew[0:E // w * w].rearrange("(a b) -> a b", b=w)).then_inc(lists_in, 16)
            sp.dma_start(list_w[E // w:E // w + 1, 0:E % w], ew[E // w * w:E].rearrange("(a b) -> a b", a=1)).then_inc(lists_in, 16)
            consts = [(w1s[:, :], m1_w1[0:128, :]), (w1d[:, :], m1_w1[128:256, :]), (w1e[:, :], m1_w1[256:320, :]),
                      (w2c[:, :, :], m1_w2.rearrange("(c p) n -> p c n", p=128)), (l1w[:, :], l1_w), (gw1[:, :], g_w1),
                      (gw2[:, :, :], g_w2.rearrange("(c p) n -> p c n", p=128)), (l3w[:, :], l3_w)]
            consts += [(to[:, :], of.rearrange("(a n) -> a n", a=1).to_broadcast([128, 128]))
                       for to, of in ((l1b, l1_b), (gb2, g_b2), (l3b, l3_b))]
            for to, of in consts:
                sp.dma_start(to, of).then_inc(loads, 16)
            with nc.allow_non_contiguous_dma(reason="bias vectors as columns, once"):
                sp.dma_start(b1c[:, :], m1_b1.rearrange("(c p) -> p c", p=128)).then_inc(loads, 16)
                sp.dma_start(gb1[:, :], g_b1.rearrange("(c p) -> p c", p=128)).then_inc(loads, 16)
            sp.wait_ge(bias_rows_zeroed, 2)
            for j, of in enumerate((l1_b, l3_b, m1_b2)):
                for p in (0, 32):
                    sp.dma_start(bias_rows[p:p + 1, j, :], of.rearrange("(a n) -> a n", a=1)).then_inc(loads, 16)
            assert len(consts) + 8 == n_const
            sp.wait_ge(lists_float, 1)
            for j, to in enumerate((src_pad, dst_pad)):
                sp.dma_start(to.rearrange("(a b) -> a b", b=w), list_f[:, j, :]).then_inc(lists_out, 16)
            in_blocks = blocks[0:EP // BLOCK, :, :].rearrange("(a r) j b -> a r j b", a=112)
            for j, of in enumerate((list_f[:, 0, :], list_f[:, 1, :], list_w[:, :])):
                sp.dma_start(in_blocks[:, :, j, :], of.rearrange("a (r b) -> a r b", b=BLOCK)).then_inc(blocks_out, 16)
            sp.dma_start(blocks[EP // BLOCK:, :, :].rearrange("a j b -> a (j b)"), last_blocks[:, :, :].rearrange("a j b -> a (j b)")).then_inc(blocks_out, 16)
            sp.wait_ge(lists_out, 32)
            sp.wait_ge(spare_set, 4)
            for tab, of in ((src_f, src_pad), (dst_f, dst_pad)):
                sp.dma_start(tab[:, 0:EP // 128].rearrange("p (c k) -> p c k", k=2),
                             of.rearrange("(c p k) -> p c k", p=128, k=2)).then_inc(tables, 16)
            wv = w_f[:, :].rearrange("p (c k) -> p c k", k=2)
            sp.dma_start(wv[:, 0:full // 256, :], ew[0:full].rearrange("(c p k) -> p c k", p=128, k=2)).then_inc(tables, 16)
            sp.dma_start(wv[0:rest, full // 256, :], ew[full:E].rearrange("(p k) -> p k", k=2)).then_inc(tables, 16)
            sp.wait_ge(zero_ready, 2)
            for to, wd in ((x1, D), (d1, DW), (s2, D), (t2, D), (s3, D)):
                sp.dma_start(to[DUMMY:NR, :].rearrange("(p r) f -> p (r f)", r=4), zero[:, 0:4 * wd]).then_inc(dummies_set, 16)

            def load_idx_row(e, of, t):
                wait_past(sp, e.row_read, t.n - 1)
                sp.dma_start(idx_row[:, t.slot(), :], of[bass.ds(t.n * 512, 512)].rearrange("(a n) -> a n", a=1).to_broadcast([128, 512]))\
                    .then_inc(e.row_loaded[t.slot()], 16)

            def load_attributes(t):
                wait_past(sp, turned, 3 * (t.n - 1))
                to = eav[:, t.slot(), :, :].rearrange("p (b k) f -> p b (k f)", k=2)
                if last_turn(t):
                    flat = ea_flat[t.n * 512 * 64:E * 64]
                    sp.dma_start(to[:, 0, :], flat[0:256 * 64].rearrange("(p j) -> p j", p=128)).then_inc(ea_loaded[t.slot()], 16)
                    sp.dma_start(to[0:rest, 1, :], flat[256 * 64:].rearrange("(p j) -> p j", p=rest)).then_inc(ea_loaded[t.slot()], 16)
                else:
                    of = ea_flat[bass.ds(t.n * (512 * 64), 512 * 64)]
                    sp.dma_start(to, of.rearrange("(b p j) -> p b j", b=2, p=128)).then_inc(ea_loaded[t.slot()], 16)

            def mlp_loads(at):
                if at(0):
                    load_attributes(at(0))
                if at(1):
                    load_idx_row(mlp, src_pad, at(1))

            run(sp, Part(EDGE_TURNS - 1, 1, mlp_loads))
            load_attributes(Turn(None, EDGE_TURNS - 1))
            load_idx_row(mlp, src_pad, Turn(None, EDGE_TURNS - 1))

            def set_targets():
                sp.wait_ge(d1_row_ready, 1)

                def step(at):
                    for to, of in ((d1, d1_row[:, :, :].rearrange("p r f -> p (r f)")), (s3, zero[:, :])):
                        sp.dma_start(to[bass.ds(at(0).n * 1024, 1024), :].rearrange("(p r) f -> p (r f)", r=8), of).then_inc(targets_set, 16)
                run(sp, Part(EDGE_TURNS, 0, step))

            def idx_rows(e):
                return Part(EDGE_TURNS, 0, lambda at: load_idx_row(e, dst_pad, at(0)))

            def row_slots_free(e):
                return lambda: sp.wait_ge(e.row_read, EDGE_TURNS)

            def node_io(flow, inputs_read, ins, outs, sums=None):
                def step(at):
                    new = at(0)
                    if new:
                        if sums and new.first():
                            sp.wait_ge(sums.scattered, 64 * EDGE_TURNS)
                        wait_past(sp, inputs_read, new.n - 3)
                        for of, buf in ins:
                            sp.dma_start(buf[:, new.slot(4), 0:4 * of.shape[1]], nodes(of, new.n)).then_inc(node_loaded[new.slot(4)], 16)
                    for to, buf, result, lag in outs:
                        old = at(lag)
                        if old:
                            sp.wait_ge(result, old.n + 1)
                            if to is out and old.i is None and old.n == NODE_TURNS - 1:
                                sp.dma_start(nodes(out, old.n, last_rows), buf[0:last_rows // 4, old.slot(4), :]).then_inc(node_stored[old.slot(4)], 16)
                            else:
                                sp.dma_start(nodes(to, old.n), buf[:, old.slot(4), :]).then_inc(node_stored[old.slot(4)], 16)
                return Part(NODE_TURNS, max(o[3] for o in outs), step)

            def stored(flow):
                def wait():
                    for u in range(4):
                        sp.wait_ge(node_stored[u], flow.stores_done)
                return wait

            def x1_whole():
                sp.wait_ge(x1_set, 32)
                sp.wait_ge(mlp.scattered, 64 * EDGE_TURNS)

            passes(sp, set_targets, [
                (x1_whole, node_io(w_x2, n_x2.inputs_read, [(x1, na)], [(x2, nt, x2_ready, 4), (h2, no, n_x2.result, 6)])),
                (stored(w_x2), node_io(w_gcn, n_gcn.inputs_read, [(h2, na)], [(z2, no, n_gcn.result, 6)])),
                (stored(w_gcn), node_io(w_x3, n_x3.result, [(z2, na), (x2, nb)], [(x3, no, n_x3.result, 4)])),
                (stored(w_x3), node_io(w_out, n_out.result, [(x3, na)], [(out, no, n_out.result, 4)])),
                (stored(w_out), None),
            ], [
                (row_slots_free(mlp), idx_rows(wag),
                 node_io(n_x2, n_x2.inputs_read, [(x1, na), (d1, nb)],
                         [(x2, nt, x2_ready, 4), (h2, no, n_x2.result, 4), (s2, no, n_x2.result, 4)], wag)),
                (row_slots_free(wag), idx_rows(gc1),
                 node_io(n_gcn, n_gcn.inputs_read, [(s2, na)], [(z2, no, n_gcn.result, 4), (t2, no, n_gcn.result, 4)], gc1)),
                (row_slots_free(gc1), idx_rows(gc2), node_io(n_x3, n_x3.result, [(x2, na), (t2, nb)], [(x3, no, n_x3.result, 4)], gc2)),
                (row_slots_free(gc2), idx_rows(gra), node_io(n_out, n_out.result, [(x3, na), (s3, nb)], [(out, no, n_out.result, 4)], gra)),
                (stored(n_out), None),
            ])

        @block.gpsimd
        def _(pool):
            G = nc.gpsimd
            G.memset(list_i[:, :, :], PAD_INDEX).then_inc(pad_ready, 1)
            G.memset(list_w[:, :], 0.0).then_inc(pad_ready, 1)
            G.memset(last_blocks[:, 0:2, :], float(PAD_INDEX)).then_inc(pad_ready, 1)
            G.iota(first_node_i[:, :], [[512, NODE_TURNS + 1]], base=0, channel_multiplier=0).then_inc(win_iotas, 1)
            G.iota(block_no_i[:, :], [[1, BLOCKS]], base=0, channel_multiplier=0).then_inc(win_iotas, 1)
            G.iota(base_i[:, :, :], [[512, NODE_TURNS], [0, TILES]], base=0, channel_multiplier=0).then_inc(win_iotas, 1)
            G.iota(node_no_i[:, :], [[1, 4], [4, 128]], base=0, channel_multiplier=0).then_inc(win_iotas, 1)
            G.memset(zero[:, :], 0.0).then_inc(zero_ready, 1)
            G.memset(eps_c[:, :], EPS).then_inc(zero_ready, 1)
            G.memset(ident[:, :], 0.0).then_inc(ready, 1)
            G.memset(rank[:, :, :], 1.0).then_inc(ready, 1)
            pool.wait_ge(ready, 2)
            G.affine_select(out=ident[:, :], in_=ident[:, :], compare_op=ALU.not_equal, fill=1.0, base=0,
                            pattern=[[-1, 128]], channel_multiplier=1).then_inc(ready, 1)
            for s in range(4):
                place = dict(base=256 * (s // 2) + s % 2, pattern=[[-1, 512]], channel_multiplier=2)
                G.affine_select(out=rank[:, s, :], in_=rank[:, s, :], compare_op=ALU.is_ge, fill=LATER, **place).then_inc(ready, 1)
                pool.wait_ge(ready, 4 + 2 * s)
                G.affine_select(out=rank[:, s, :], in_=rank[:, s, :], compare_op=ALU.not_equal, fill=0.0, **place).then_inc(ready, 1)
            G.iota(dummy_i[:, :], [[128, 4]], base=DUMMY, channel_multiplier=1).then_inc(ready, 1)

            def gate(*waits):
                for s, v in waits:
                    wait_past(pool, s, v)
                pool.sem_inc(gates, 1)

            def edge_step(e, of, tiles, rows_read, to, buf, lag, target_set):
                def step(at):
                    new, old = at(0), at(lag)
                    if new:
                        gate((e.gidx_ready, new.n + 1), (rows_read, new.n - 1))
                        for s in range(tiles):
                            pool.indirect_dma_start(rows[:, new.slot(), s, :], None, of,
                                                    bass.IndirectOffsetOnAxis(ap=gidx[:, new.slot(), s:s + 1], axis=0))\
                                .then_inc(e.gathered[new.slot()], 16)
                    if old:
                        gate((e.out_ready, old.n + 1), (e.sidx_ready, old.n + 1))
                        if old.first():
                            for s, v in target_set:
                                gate((s, v))
                        else:
                            gate((e.scattered, 64 * old.n))
                        for s in range(4):
                            pool.indirect_dma_start(to, bass.IndirectOffsetOnAxis(ap=sidx[:, old.slot(), s:s + 1], axis=0),
                                                    buf[:, old.slot(), s, :], None, compute_op=ALU.add).then_inc(e.scattered, 16)
                return step, lag

            def gather_window_blocks():
                gate((blocks_out, 64), (window_block_set, 2))
                for h, buf in enumerate((na, nt)):
                    to = buf[0:HALF, :, :].rearrange("g u f -> g (u f)")
                    for j in range(BLOCKS):
                        pool.indirect_dma_start(to[:, 3 * BLOCK * j:3 * BLOCK * (j + 1)], None,
                                                blocks[:, :, :].rearrange("a j b -> a (j b)"),
                                                bass.IndirectOffsetOnAxis(ap=window_block[:, h, j:j + 1], axis=0))\
                            .then_inc(blocks_in, 16)

            gather_window_blocks()
            step, lag = edge_step(mlp, x, 8, mlp.xn_ready, x1, mout, 5, [(x1_set, 32), (dummies_set, 80)])
            run(pool, Part(EDGE_TURNS, lag, step))

            def whole(flow):
                def wait():
                    for u in range(4):
                        gate((node_stored[u], flow.stores_done))
                return wait

            def gathers(w, of, rows_read):
                def step(at):
                    t = at(0)
                    gate((w.gidx_ready, t.n + 1), (rows_read, t.n - 3))
                    for s in range(TILES):
                        pool.indirect_dma_start(rows4(t)[:, s, :], None, of,
                                                bass.IndirectOffsetOnAxis(ap=wgidx[:, t.slot(4), s:s + 1], axis=0))\
                            .then_inc(w.gathered[t.slot(4)], 16)
                return Part(NODE_TURNS, 0, step)

            def batches(e, of, rows_read, to, buf, target_set):
                step, lag = edge_step(e, of, 4, rows_read, to, buf, 3, target_set)
                return Part(EDGE_TURNS, lag, step)

            x1_whole = lambda: gate((mlp.scattered, 64 * EDGE_TURNS))
            passes(pool, nothing, [
                (x1_whole, gathers(w_x2, x1, wag.xn_ready)),
                (whole(w_x2), gathers(w_gcn, h2, split_ready)),
                (whole(w_gcn), gathers(w_x3, z2, gc2.summed)),
                (whole(w_x3), gathers(w_out, x3, gra.xn_ready)),
            ], [
                (x1_whole, batches(wag, x1, wag.xn_ready, d1, dout, [(targets_set, 32 * EDGE_TURNS)])),
                (whole(n_x2), batches(gc1, h2, gc1.summed, s2, mout, [])),
                (whole(n_gcn), batches(gc2, z2, gc2.summed, t2, mout, [])),
                (whole(n_x3), batches(gra, x3, gra.xn_ready, s3, mout, [])),
            ])

        @block.vector
        def _(dve):
            V = nc.vector
            V.memset(bias_rows[:, :, :], 0.0).then_inc(bias_rows_zeroed, 1)
            V.memset(bias_split[:, :, :], 0.0).then_inc(bias_rows_zeroed, 1)
            V.memset(w_f[:, :], 0.0).then_inc(spare_set, 1)
            V.memset(src_f[:, EP // 128:], 0.0).then_inc(spare_set, 1)
            V.memset(dst_f[:, EP // 128:], 0.0).then_inc(spare_set, 1)
            V.memset(last_blocks[:, 2, :], 0.0).then_inc(spare_set, 1)
            V.memset(win_src[:, NODE_TURNS:, :], 0.0).then_inc(counted, 1)
            V.memset(ones[:, :], 1.0).then_inc(counted, 1)
            V.memset(up_col[:, :], 0.0).then_inc(counted, 1)
            V.memset(over_col[:, :], 0.0).then_inc(counted, 1)
            V.memset(dout[:, :, :, :], 0.0).then_inc(tables_f, 1)
            V.memset(d1_row[:, :, :], 0.0).then_inc(tables_f, 1)
            dve.wait_ge(lists_in, 8 * 16)
            V.tensor_copy(list_f[:, :, :], list_i[:, :, :]).then_inc(lists_float, 1)
            dve.wait_ge(win_iotas, 4)
            V.tensor_copy(first_node[:, :], first_node_i[:, :]).then_inc(counted, 1)
            dve.wait_ge(counted, 5)
            dve.wait_ge(lists_float, 1)

            def count_below(g, slot):
                V.scalar_tensor_tensor(out=eq[0:112, slot // 4, slot % 4, 0:LIST].bitcast(F32R), in0=list_f[:, 1, :], scalar=first_node[:, bass.ds(g, 1)],
                                       in1=ones[0:112, 0:1].to_broadcast([112, LIST]), op0=ALU.is_lt, op1=ALU.mult,
                                       accum_out=below[:, bass.ds(g, 1)]).then_inc(below_steps, 1)
            peeled = (NODE_TURNS + 1) % 8
            for g in range(peeled):
                count_below(g, g)
            with dve.Fori(0, (NODE_TURNS + 1) // 8) as i:
                dve.wait_ge(below_steps, i * 8 + peeled)
                for u in range(8):
                    count_below(i * 8 + peeled + u, u)
            dve.wait_ge(below_steps, NODE_TURNS + 1)
            dve.sem_inc(counted, 1)
            V.tensor_tensor(step_up[:, :], list_f[:, 2, :], list_f[:, 1, :], ALU.subtract).then_inc(start_steps, 1)
            V.tensor_copy(block_no[:, :], block_no_i[:, :]).then_inc(start_steps, 1)
            V.tensor_copy(base_f[:, :, :], base_i[:, :, :]).then_inc(start_steps, 1)
            V.tensor_copy(node_no[:, :], node_no_i[:, :]).then_inc(start_steps, 1)
            dve.wait_ge(start_steps, 4)
            V.tensor_reduce(up_col[0:112, :], step_up[:, :], AX.X, ALU.min).then_inc(start_steps, 1)
            dve.wait_ge(counts_psum, 1)
            V.tensor_copy(start[:, :, :], bank[6][0:HALF, 0:4].rearrange("g (h n) -> g h n", n=2)).then_inc(start_steps, 1)
            dve.wait_ge(start_steps, 6)
            V.tensor_copy(start_i[:, :], start[:, :, 0]).then_inc(start_steps, 1)
            dve.wait_ge(start_steps, 7)
            V.tensor_scalar(block_i[:, :], start_i[:, :], BLOCK.bit_length() - 1, None, ALU.arith_shift_right).then_inc(start_steps, 1)
            dve.wait_ge(start_steps, 8)
            V.tensor_copy(block_f[:, :], block_i[:, :]).then_inc(start_steps, 1)
            dve.wait_ge(start_steps, 9)
            for h in range(2):
                V.tensor_scalar(window_block[:, h, :], block_no[:, :], block_f[:, h:h + 1], None, ALU.add).then_inc(window_block_set, 1)
            V.scalar_tensor_tensor(out=over[:, :], in0=block_f[:, :], scalar=float(BLOCK), in1=start[:, :, 1],
                                   op0=ALU.mult, op1=ALU.subtract).then_inc(start_steps, 1)
            dve.wait_ge(start_steps, 10)
            V.tensor_reduce(over[:, 0:1], over[:, :], AX.X, ALU.min).then_inc(start_steps, 1)
            dve.wait_ge(start_steps, 11)
            V.tensor_scalar(over_col[0:HALF, :], over[:, 0:1], float(WINDOW), None, ALU.add).then_inc(start_steps, 1)
            dve.wait_ge(start_steps, 12)
            V.tensor_tensor(lag_col[:, :], over_col[:, :], up_col[:, :], ALU.min).then_inc(lag_ready, 1)
            dve.wait_ge(loads, 16 * n_const)
            dve.wait_ge(tables_f, 2)
            V.tensor_copy(d1_row[:, :, 0:D], l1b[:, :].rearrange("p (a f) -> p a f", a=1).to_broadcast([128, 8, D])).then_inc(d1_row_ready, 1)
            V.tensor_copy(bias_high[:, :, :].bitcast(F32R), bias_rows[:, :, :]).then_inc(bias_rows_zeroed, 1)
            dve.wait_ge(bias_rows_zeroed, 3)
            V.tensor_copy(bias_split[0:1, :, :].bitcast(F32R), bias_high[0:1, :, :])
            V.tensor_tensor(bias_split[32:33, :, :].bitcast(F32R), bias_rows[32:33, :, :], bias_high[32:33, :, :], ALU.subtract)
            dve.wait_ge(ready, 12)
            V.tensor_copy(dummy_f[:, :], dummy_i[:, :]).then_inc(tables_f, 1)
            dve.wait_ge(wT_psum, 1)
            V.tensor_copy(l1wT[:, :], bank[0][:, 0:128]).then_inc(wT_out, 1)
            dve.wait_ge(lag_psum, 1)
            V.tensor_reduce(lag_min[:, :], bank[7][0:1, 0:128], AX.X, ALU.min).then_inc(tables_f, 1)
            dve.wait_ge(tables_f, 4)
            V.tensor_scalar(ascends[:, :], lag_min[:, :], 0.0, None, ALU.is_ge).then_inc(flag_ready, 1)

            dve.wait_ge(blocks_in, 2 * BLOCKS * 16)
            for of, to in ((na, nb), (nt, no)):
                V.tensor_copy(window_lists(to).rearrange("g (l j b) -> g l j b", l=3, b=BLOCK),
                              window_lists(of).rearrange("g (j l b) -> g l j b", l=3, b=BLOCK)).then_inc(window_lists_set, 1)
            n = 0
            for h in range(2):
                for tab in (win_src, win_dst, win_w):
                    for s in range(TILES):
                        dve.wait_ge(win_psum, n + 1)
                        V.tensor_copy(tab[:, HALF * h:HALF * (h + 1), s], bank[n % 4][:, 0:HALF]).then_inc(win_out, 1)
                        n += 1
            dve.wait_ge(win_out, 6 * TILES)
            V.tensor_tensor(win_key[:, :, :], win_dst[:, :, :], base_f[:, :, :], ALU.subtract).then_inc(start_steps, 1)
            dve.wait_ge(start_steps, 13)
            dve.wait_ge(tables, 64)

            def cols(t, n):
                return t[:, bass.ds(n * 4, 4)]

            def copy_cols(to, of):
                return V.tensor_scalar(to, of, 1.0, None, ALU.mult)

            def set_gidx(e, n, slot, tabs):
                for j, tab in enumerate(tabs):
                    ins = V.tensor_scalar(gidx[:, slot, 4 * j:4 * j + 4], cols(tab, n), float(N - 1), None, ALU.min)
                ins.then_inc(e.gidx_ready, 1)

            def set_next_gidx(e, new, tabs):
                wait_past(dve, e.gathered[1 - new.slot()], 64 * len(tabs) * (new.use() + new.slot()))
                set_gidx(e, new.n + 1, 1 - new.slot(), tabs)

            def row_stats(steps, count, rows_of, st, mean_var, between=None):
                for s in range(count):
                    steps.inc(V.bn_stats(st[:, s, :], rows_of(s)))
                steps.wait()
                between()
                for s in range(count):
                    ins = V.bn_aggr(mean_var[:, s, :], st[:, s, :])
                return ins

            def scale_and_bias(e, steps, t, count):
                dve.wait_ge(e.sd_ready, t.n + 1)
                steps.inc(V.reciprocal(rstd[:, t.slot(), 0:count], sd[:, t.slot(), 0:count]))
                steps.wait()
                V.scalar_tensor_tensor(out=nmr[:, t.slot(), 0:count], in0=mv[:, t.slot(), 0:count, 0], scalar=-1.0,
                                       in1=rstd[:, t.slot(), 0:count], op0=ALU.mult, op1=ALU.mult).then_inc(e.norm_ready, 1)

            def equalities(t):
                for s in range(4):
                    ins = V.tensor_scalar(eq[:, t.slot(), s, :].bitcast(F32R).rearrange("q (b k p) -> q b k p", k=2, p=128),
                                          idx_row[:, t.slot(), :].rearrange("q (b p k) -> q b k p", k=2, p=128),
                                          key[:, t.slot(), s:s + 1], None, ALU.is_equal)
                return ins

            def leaders(steps, t):
                for s in range(4):
                    steps.inc(V.scalar_tensor_tensor(out=junk[:, s, :], in0=idx_row[:, t.slot(), :],
                                                     scalar=key[:, t.slot(), s:s + 1], in1=rank[:, s, :],
                                                     op0=ALU.is_equal, op1=ALU.mult, accum_out=cnt[:, s:s + 1]))
                steps.inc(V.tensor_tensor(off[:, :], dummy_f[:, :], key[:, t.slot(), :], ALU.subtract))
                steps.wait()
                steps.inc(V.scalar_tensor_tensor(out=off2[:, :], in0=cnt[:, :], scalar=LATER, in1=off[:, :], op0=ALU.is_ge, op1=ALU.mult))
                steps.wait()
                return V.tensor_tensor(sidx[:, t.slot(), :], off2[:, :], key[:, t.slot(), :], ALU.add)

            steps = Steps(dve, mlp.dve, 8 + 1)
            lead = Steps(dve, mlp.dve_lead, 1 + 6)
            set_gidx(mlp, 0, 0, (src_f, dst_f))

            def mlp_step(at):
                new, t = at(0), at(3)
                if new:
                    set_next_gidx(mlp, new, (src_f, dst_f))
                if t:
                    dve.wait_ge(msg_high, t.n + 1)
                    V.tensor_tensor(low[:, t.slot(), :, :].bitcast(F32R), by4(bank[5][:, :]), high[:, t.slot(), :, :], ALU.subtract)\
                        .then_inc(msg_split, 1)
                if new:
                    steps.begin(new)
                    dve.wait_ge(mlp.gathered[new.slot()], 128 * (new.use() + 1))
                    row_stats(steps, 8, lambda s: rows[:, new.slot(), s, :], stats, mv[:, new.slot(), :, :],
                              lambda: t and lead_key(t)).then_inc(mlp.var_ready, 1)
                elif t:
                    lead_key(t)
                if t:
                    dve.wait_ge(mlp.row_loaded[t.slot()], 16 * (t.use() + 1))
                    wait_past(dve, mlp.summed, t.n - 1)
                    lead.wait()
                    equalities(t).then_inc(mlp.eq_ready, 1)
                if new:
                    scale_and_bias(mlp, steps, new, 8)
                    steps.end()
                if t:
                    wait_past(dve, mlp.scattered, 64 * (t.n - 1))
                    leaders(lead, t).then_inc(mlp.sidx_ready, 1)
                    dve.wait_ge(mlp.sidx_ready, t.n + 1)
                    dve.sem_inc(mlp.row_read, 1)
                    lead.end()

            def lead_key(t):
                lead.begin(t)
                lead.inc(copy_cols(key[:, t.slot(), :], cols(src_f, t.n)))

            run(dve, Part(EDGE_TURNS, 3, mlp_step))

            def sums_landed(e, then):
                def prepare():
                    dve.wait_ge(e.scattered, 64 * EDGE_TURNS)
                    set_gidx(then, 0, 0, (src_f,))
                return prepare

            def wag_step(at):
                new, old = at(0), at(1)
                if new:
                    wsteps.begin(new)
                    set_next_gidx(wag, new, (src_f,))
                if old:
                    wlead.begin(old)
                    wait_past(dve, wag.scattered, 64 * (old.n - 1))
                    leaders(wlead, old).then_inc(wag.sidx_ready, 1)
                    wlead.inc(V.tensor_scalar(dout[:, old.slot(), :, D], cnt[:, :], 1.0, None, ALU.add))
                    dve.wait_ge(wag.sidx_ready, old.n + 1)
                    copy_cols(cols(leader, old.n), sidx[:, old.slot(), :]).then_inc(wag.row_read, 1)
                    wlead.end()
                if new:
                    dve.wait_ge(wag.gathered[new.slot()], 64 * (new.use() + 1))
                    row_stats(wsteps, 4, lambda s: rows[:, new.slot(), s, :], stats, mv[:, new.slot(), :, :],
                              lambda: wsteps.inc(copy_cols(key[:, new.slot(), :], cols(dst_f, new.n)))).then_inc(wag.var_ready, 1)
                if old:
                    wait_past(dve, aggT_psum, old.n)
                    dve.wait_ge(wag.xn_ready, old.n + 1)
                    V.tensor_tensor(xw[:, 0, :, :], xn[:, 0:4, :], each4(w_f, old.n), ALU.mult).then_inc(xw_ready, 1)
                if new:
                    dve.wait_ge(wag.row_loaded[new.slot()], 16 * (new.use() + 1))
                    wait_past(dve, wag.summed, new.n - 1)
                    wsteps.wait()
                    equalities(new).then_inc(wag.eq_ready, 1)
                    scale_and_bias(wag, wsteps, new, 4)
                    wsteps.end()

            wsteps = Steps(dve, wag.dve, 4 + 1 + 1)
            wlead = Steps(dve, wag.dve_lead, 6 + 1)

            xsteps = Steps(dve, n_x2.dve, 4)
            xsteps2 = Steps(dve, x2_norm_steps, 3)

            def x2_step(at):
                new, old = at(0), at(1)
                if new:
                    s, s4 = new.slot(), new.slot(4)
                    xsteps.begin(new)
                    dve.wait_ge(node_loaded[s4], n_x2.loaded(new))
                    wait_past(dve, node_stored[s4], n_x2.slot_stored(new))
                    V.tensor_tensor(by4(nt[:, s4, :]), by4(na[:, s4, :]), by4(nb[:, s4, :])[:, :, 0:D], ALU.add)\
                        .then_inc(x2_ready, 1)
                    dve.wait_ge(x2_ready, new.n + 1)
                    row_stats(xsteps, 4, lambda k: nt[:, s4, 128 * k:128 * k + 128], nstats, nmv[:, s, :, :],
                              lambda: V.tensor_copy(degree[:, s, :], by4(nb[:, s4, :])[:, :, D])).then_inc(n_x2.inputs_read, 1)
                    xsteps.end()
                if old:
                    x2_scale(old)

            def x2_scale(t):
                s = t.slot()
                xsteps2.begin(t)
                dve.wait_ge(nsd_ready, t.n + 1)
                wait_past(dve, n_x2.result, t.n - 1)
                xsteps2.inc(V.reciprocal(nrsd[:, s, :], nsd[:, s, :]))
                xsteps2.wait()
                xsteps2.inc(V.tensor_tensor(nrstd[:, s, :], nrsd[:, s, 0:4], nrsd[:, s, 4:8], ALU.mult))
                xsteps2.inc(copy_cols(cols(dinv, t.n), nrsd[:, s, 4:8]))
                xsteps2.wait()
                V.scalar_tensor_tensor(out=nnmr[:, s, :], in0=nmv[:, s, :, 0], scalar=-1.0, in1=nrstd[:, s, :],
                                       op0=ALU.mult, op1=ALU.mult).then_inc(x2_norm, 1)
                xsteps2.end()

            def plain_edges(e, norm):
                psteps = Steps(dve, e.dve, 1 + (5 if norm else 0))

                def step(at):
                    t, old = at(0), at(1)
                    if old:
                        wait_past(dve, e.scattered, 64 * (old.n - 1))
                        copy_cols(sidx[:, old.slot(), :], cols(leader, old.n)).then_inc(e.sidx_ready, 1)
                    if not t:
                        return

                    def keys():
                        psteps.inc(copy_cols(key[:, t.slot(), :], cols(dst_f, t.n)))
                    psteps.begin(t)
                    set_next_gidx(e, t, (src_f,))
                    if norm:
                        dve.wait_ge(e.gathered[t.slot()], 64 * (t.use() + 1))
                        row_stats(psteps, 4, lambda s: rows[:, t.slot(), s, :], stats, mv[:, t.slot(), :, :], keys).then_inc(e.var_ready, 1)
                    else:
                        keys()
                    dve.wait_ge(e.row_loaded[t.slot()], 16 * (t.use() + 1))
                    wait_past(dve, e.summed, t.n - 1)
                    psteps.wait()
                    equalities(t).then_inc(e.eq_ready, 1)
                    if norm:
                        scale_and_bias(e, psteps, t, 4)
                    dve.wait_ge(e.eq_ready, t.n + 1)
                    dve.sem_inc(e.row_read, 1)
                    psteps.end()
                return Part(EDGE_TURNS, 1, step)

            def gcn_step(at):
                new, mid, old = at(0), at(1), at(2)
                if new:
                    s4 = new.slot(4)
                    dve.wait_ge(node_loaded[s4], n_gcn.loaded(new))
                    wait_past(dve, n_gcn.turned, new.n - 3)
                    V.tensor_tensor(by4(nt[:, s4, :]), by4(na[:, s4, :]), each4(dinv, new.n), ALU.mult)\
                        .then_inc(n_gcn.inputs_read, 1)
                if old:
                    z2_out(n_gcn, old)
                if mid:
                    hidden_half(mid)

            def z2_out(flow, t):
                s4 = t.slot(4)
                dve.wait_ge(n_gcn.product, t.n + 1)
                wait_past(dve, node_stored[s4], flow.slot_stored(t))
                V.tensor_tensor(by4(no[:, s4, :]), by4(bank[5][:, :]), each4(dinv, t.n), ALU.mult).then_inc(n_gcn.result, 1)

            def hidden_half(t):
                for c in (2, 3):
                    dve.wait_ge(ghid_psum, 4 * t.n + c + 1)
                    V.tensor_scalar(nhid[:, c, :], bank[1 + c][:, :], gb1[:, c:c + 1], 0.0, ALU.add, ALU.max)\
                        .then_inc(ghid_dve, 1)

            x3steps = Steps(dve, n_x3.dve, 2)

            def x3_step(at):
                t, s4 = at(0), at(0).slot(4)
                x3steps.begin(t)
                dve.wait_ge(node_loaded[s4], n_x3.loaded(t))
                x3steps.inc(V.tensor_tensor(by4(ntmp[:, 0, :]), by4(nb[:, s4, 0:512]), each4(dinv, t.n), ALU.mult))
                x3steps.wait()
                x3steps.inc(V.tensor_tensor(by4(ntmp[:, 1, :]), by4(ntmp[:, 0, :]), row4(gb2), ALU.add))
                x3steps.wait()
                wait_past(dve, node_stored[s4], n_x3.slot_stored(t))
                V.scalar_tensor_tensor(out=no[:, s4, :], in0=ntmp[:, 1, :], scalar=0.0, in1=na[:, s4, :],
                                       op0=ALU.max, op1=ALU.add).then_inc(n_x3.result, 1)
                x3steps.end()

            osteps = Steps(dve, n_out.dve, 1)

            def out_step(at):
                t = at(1)
                if t:
                    s4 = t.slot(4)
                    osteps.begin(t)
                    dve.wait_ge(n_out.product, t.n + 1)
                    osteps.inc(V.tensor_tensor(by4(ntmp[:, 0, :]), by4(bank[1][:, :]), row4(l3b), ALU.add))
                    osteps.wait()
                    wait_past(dve, node_stored[s4], n_out.slot_stored(t))
                    V.scalar_tensor_tensor(out=no[:, s4, :], in0=ntmp[:, 0, :], scalar=0.0, in1=na[:, s4, :],
                                           op0=ALU.max, op1=ALU.add).then_inc(n_out.result, 1)
                    osteps.end()

            def start_windows(w, after=None):
                def prepare():
                    if after:
                        after()
                    for n in range(3):
                        window_gidx(w, n, n)
                return prepare

            def window_gidx(w, n, slot):
                V.tensor_scalar(wgidx[:, slot, :], win_src[:, bass.ds(n, 1), :].rearrange("p a s -> p (a s)"), float(N - 1), None, ALU.min)\
                    .then_inc(w.gidx_ready, 1)

            def next_window_gidx(w, t):
                slot = (t.slot(4) + 3) % 4
                wait_past(dve, w.gathered[slot], 16 * TILES * (t.use(4) + (t.slot(4) > 0)))
                window_gidx(w, t.n + 3, slot)

            def one_hot(w, t):
                wait_past(dve, w.summed, t.n - 1)
                for s in range(TILES):
                    ins = V.tensor_scalar(eq[:, t.slot(), s, :].bitcast(F32R), node_no[:, :], win(win_key, t)[:, s:s + 1], None, ALU.is_equal)
                ins.then_inc(w.eq_ready, 1)

            def window_stats(w, steps, t):
                dve.wait_ge(w.gathered[t.slot(4)], 16 * TILES * (t.use(4) + 1))
                row_stats(steps, TILES, lambda s: rows4(t)[:, s, :], stats, mv[:, t.slot(), :, :],
                          lambda: next_window_gidx(w, t)).then_inc(w.e.var_ready, 1)

            w1steps = Steps(dve, wag.dve, TILES)
            w1steps2 = Steps(dve, wag.dve_lead, 1)

            def w_x2_step(at):
                new, one, two, four = at(0), at(1), at(2), at(4)
                if one:
                    w1steps2.begin(one)
                    scale_and_bias(wag, w1steps2, one, TILES)
                    w1steps2.end()
                if new:
                    w1steps.begin(new)
                    window_stats(w_x2, w1steps, new)
                    w1steps.end()
                if two:
                    one_hot(w_x2, two)
                    dve.wait_ge(wag.xn_ready, two.n + 1)
                    weight = win(win_w, two).rearrange("p (s a) -> p s a", a=1).to_broadcast([128, TILES, 128])
                    V.tensor_tensor(xw[:, two.slot(), 0:TILES, :], xn2(two)[:, 0:TILES, :], weight, ALU.mult).then_inc(xw_ready, 1)
                if at(5):
                    x2_scale(at(5))
                if four:
                    s, s4 = four.slot(), four.slot(4)
                    xsteps.begin(four)
                    dve.wait_ge(node_loaded[s4], w_x2.loaded(four))
                    dve.wait_ge(product, four.n + 1)
                    wait_past(dve, node_stored[s4], w_x2.slot_stored(four))
                    V.tensor_tensor(nt[:, s4, :], na[:, s4, :], bank[2 + s][:, :], ALU.add).then_inc(x2_ready, 1)
                    dve.wait_ge(x2_ready, four.n + 1)
                    row_stats(xsteps, 4, lambda k: nt[:, s4, 128 * k:128 * k + 128], nstats, nmv[:, s, :, :],
                              lambda: V.tensor_copy(degree[:, s, :], bank[4 + s4][:, 0:8].rearrange("p (q a) -> p q a", a=2)[:, :, 0])).then_inc(n_x2.inputs_read, 1)
                    xsteps.end()

            def plain_windows(w, node_first, node_last, lag, eq_lag=0):
                def step(at):
                    node_first(at)
                    if at(0):
                        next_window_gidx(w, at(0))
                    if at(eq_lag):
                        one_hot(w, at(eq_lag))
                    node_last(at)
                return Part(NODE_TURNS, lag, step)

            def w_gcn_first(at):
                if at(6):
                    z2_out(w_gcn, at(6))
                if at(5):
                    hidden_half(at(5))
                if at(1):
                    t = at(1)
                    split.begin(t)
                    dve.wait_ge(w_gcn.gathered[t.slot(4)], 16 * TILES * (t.use(4) + 1))
                    wait_past(dve, gc1.summed, t.n - 1)
                    split.inc(V.tensor_scalar(high[:, t.slot(), 0:TILES, :].bitcast(F32R), rows4(t)[:, 0:TILES, :], 1.0, None, ALU.mult))
                    split.wait()
                    V.tensor_tensor(low[:, t.slot(), 0:TILES, :].bitcast(F32R), rows4(t)[:, 0:TILES, :], high[:, t.slot(), 0:TILES, :], ALU.subtract)\
                        .then_inc(split_ready, 1)
                    split.end()

            split = Steps(dve, split_steps, 1)
            gsteps = Steps(dve, gc1.dve, 1)

            def w_gcn_last(at):
                t = at(3)
                if t:
                    s4 = t.slot(4)
                    gsteps.begin(t)
                    dve.wait_ge(gc1.summed, t.n + 1)
                    dve.wait_ge(node_loaded[s4], w_gcn.loaded(t))
                    gsteps.inc(V.tensor_tensor(ntmp[:, t.slot(), :], na[:, s4, :], bank[6 + t.slot()][:, :], ALU.add))
                    gsteps.wait()
                    V.tensor_tensor(by4(nt[:, s4, :]), by4(ntmp[:, t.slot(), :]), each4(dinv, t.n), ALU.mult).then_inc(n_gcn.inputs_read, 1)
                    gsteps.end()

            w3steps = Steps(dve, n_x3.dve, 1)

            def w_x3_last(at):
                t = at(2)
                if t:
                    s4 = t.slot(4)
                    dve.wait_ge(gc2.summed, t.n + 1)
                    dve.wait_ge(node_loaded[s4], w_x3.loaded(t))
                    copy_cols(dinv_x3[:, s4, :], cols(dinv, t.n))
                    wait_past(dve, gc2.out_ready, t.n - 1)
                    V.tensor_tensor(ntmp[:, t.slot(), :], na[:, s4, :], bank[6 + t.slot()][:, :], ALU.add).then_inc(own_added, 1)
                t = at(4)
                if t:
                    scaled, biased = nT[:, t.slot(), :], nhid[:, t.slot(), :]
                    s4 = t.slot(4)
                    w3steps.begin(t)
                    dve.wait_ge(gc2.out_ready, t.n + 1)
                    wait_past(dve, n_x3.result, t.n - 1)
                    w3steps.inc(V.tensor_tensor(by4(biased), by4(scaled), row4(gb2), ALU.add))
                    w3steps.wait()
                    wait_past(dve, node_stored[s4], w_x3.slot_stored(t))
                    V.scalar_tensor_tensor(out=no[:, s4, :], in0=biased, scalar=0.0, in1=nb[:, s4, 0:512],
                                           op0=ALU.max, op1=ALU.add).then_inc(n_x3.result, 1)
                    w3steps.end()

            w4steps = Steps(dve, gra.dve, TILES)
            w4steps2 = Steps(dve, gra_scale_steps, 1)

            def w_out_step(at):
                new, one, two, four = at(0), at(1), at(2), at(4)
                if one:
                    w4steps2.begin(one)
                    scale_and_bias(gra, w4steps2, one, TILES)
                    w4steps2.end()
                if new:
                    w4steps.begin(new)
                    window_stats(w_out, w4steps, new)
                    w4steps.end()
                if two:
                    one_hot(w_out, two)
                    dve.wait_ge(gra.xn_ready, two.n + 1)
                    V.tensor_tensor(low[:, two.slot(), 0:TILES, :].bitcast(F32R), xn2(two)[:, 0:TILES, :],
                                    high[:, two.slot(), 0:TILES, :], ALU.subtract).then_inc(out_split, 1)
                if four:
                    s4 = four.slot(4)
                    dve.wait_ge(node_loaded[s4], w_out.loaded(four))
                    dve.wait_ge(n_out.product, four.n + 1)
                    wait_past(dve, node_stored[s4], w_out.slot_stored(four))
                    V.scalar_tensor_tensor(out=no[:, s4, :], in0=bank[2 + four.slot()][:, :], scalar=0.0, in1=na[:, s4, :],
                                           op0=ALU.max, op1=ALU.add).then_inc(n_out.result, 1)

            x1_whole = lambda: dve.wait_ge(mlp.scattered, 64 * EDGE_TURNS)
            passes(dve, nothing, [
                (start_windows(w_x2, x1_whole), Part(NODE_TURNS, 5, w_x2_step)),
                (start_windows(w_gcn), plain_windows(w_gcn, w_gcn_first, w_gcn_last, 6, 1)),
                (start_windows(w_x3), plain_windows(w_x3, lambda at: None, w_x3_last, 4)),
                (start_windows(w_out), Part(NODE_TURNS, 4, w_out_step)),
            ], [
                (sums_landed(mlp, wag), Part(EDGE_TURNS, 1, wag_step), Part(NODE_TURNS, 1, x2_step)),
                (sums_landed(wag, gc1), plain_edges(gc1, False), Part(NODE_TURNS, 2, gcn_step)),
                (sums_landed(gc1, gc2), plain_edges(gc2, False), Part(NODE_TURNS, 0, x3_step)),
                (sums_landed(gc2, gra), plain_edges(gra, True), Part(NODE_TURNS, 1, out_step)),
            ])

        @block.scalar
        def _(act):
            S = nc.scalar
            act.wait_ge(loads, 16 * n_const)
            act.wait_ge(tables, 64)
            act.dma_start(x1[0:N, :].rearrange("(a r) f -> a (r f)", a=800), x.rearrange("(a r) f -> a (r f)", a=800)).then_inc(x1_set, 16)
            act.wait_ge(zero_ready, 2)
            act.dma_start(x1[N:NP, :].rearrange("(p r) f -> p (r f)", r=4), zero[0:(NP - N) // 4, 0:4 * D]).then_inc(x1_set, 16)

            def root(e, t, count):
                act.wait_ge(e.var_ready, t.n + 1)
                S.activation(sd[:, t.slot(), 0:count], mv[:, t.slot(), 0:count, 1], ACT.Sqrt, bias=eps_c[:, :]).then_inc(e.sd_ready, 1)

            def normalise(e, t, count, func, to=xn, of=None):
                of = rows[:, t.slot(), :, :] if of is None else of
                act.wait_ge(e.norm_ready, t.n + 1)
                for s in range(count):
                    ins = S.activation(to[:, s, :], of[:, s, :], func, bias=nmr[:, t.slot(), s:s + 1],
                                       scale=rstd[:, t.slot(), s:s + 1])
                ins.then_inc(e.xn_ready, 1)

            def sums_out(e, t, of, to):
                act.wait_ge(e.summed, t.n + 1)
                wait_past(act, e.scattered, 64 * (t.n - 1))
                S.activation(to[:, t.slot(), :, 0:D], by4(of[:, :]), ACT.Copy).then_inc(e.out_ready, 1)

            def mlp_step(at):
                if at(3):
                    act.wait_ge(msg_psum, at(3).n + 1)
                    wait_past(act, mlp.summed, at(3).n - 1)
                    S.activation(high[:, at(3).slot(), :, :].bitcast(F32R), by4(bank[5][:, :]), ACT.Copy).then_inc(msg_high, 1)
                if at(0):
                    root(mlp, at(0), 8)
                if at(2):
                    for c in range(2):
                        act.wait_ge(hid_psum, 2 * at(2).n + c + 1)
                        S.activation(ehid[:, c, :], bank[3 + c][:, :], ACT.Relu, bias=b1c[:, c:c + 1]).then_inc(hid_out, 1)
                if at(1):
                    for j, (to, of, func) in enumerate(((hTs, bank[0], ACT.Relu), (hTd, bank[1], ACT.Relu), (eT, bank[2], ACT.Copy))):
                        act.wait_ge(turned, 3 * at(1).n + j + 1)
                        p = 64 if j == 2 else 128
                        S.activation(to[:, :], of[0:p, :], func).then_inc(turned_out, 1)
                if at(4):
                    sums_out(mlp, at(4), bank[6], mout)
                if at(0):
                    normalise(mlp, at(0), 8, ACT.Identity)

            run(act, Part(EDGE_TURNS, 4, mlp_step))

            def wag_step(at):
                if at(0):
                    root(wag, at(0), 4)
                if at(1):
                    act.wait_ge(aggT_psum, at(1).n + 1)
                    S.activation(hTs[:, :], bank[0][:, :], ACT.Copy).then_inc(aggT_out, 1)
                if at(0):
                    wait_past(act, xw_ready, at(0).n)
                    normalise(wag, at(0), 4, ACT.Relu)
                if at(1):
                    sums_out(wag, at(1), bank[1], dout)

            def h2_step(at):
                if at(0):
                    x2_roots(at(0))
                if at(1):
                    h2_out(n_x2, at(1))

            def x2_roots(t):
                s = t.slot()
                act.wait_ge(n_x2.inputs_read, t.n + 1)
                S.activation(nsd[:, s, 0:4], nmv[:, s, :, 1], ACT.Sqrt, bias=eps_c[:, :])
                S.activation(nsd[:, s, 4:8], degree[:, s, :], ACT.Sqrt, bias=1.0).then_inc(nsd_ready, 1)

            def h2_out(flow, t):
                s, s4 = t.slot(), t.slot(4)
                act.wait_ge(x2_norm, t.n + 1)
                wait_past(act, node_stored[s4], flow.slot_stored(t))
                for k in range(4):
                    f = slice(128 * k, 128 * k + 128)
                    ins = S.activation(no[:, s4, f], nt[:, s4, f], ACT.Relu, bias=nnmr[:, s, k:k + 1], scale=nrstd[:, s, k:k + 1])
                ins.then_inc(n_x2.result, 1)

            def plain_out(e):
                return lambda at: at(0) and sums_out(e, at(0), bank[6 + at(0).slot()], mout)

            def gcn_step(at):
                t = at(0)
                act.wait_ge(n_gcn.turned, t.n + 1)
                S.activation(nT[:, 0, :], bank[0][:, :], ACT.Copy).then_inc(n_gcn.turned_out, 1)
                hidden_half(t)

            def hidden_half(t):
                for c in range(2):
                    act.wait_ge(ghid_psum, 4 * t.n + c + 1)
                    S.activation(nhid[:, c, :], bank[1 + c][:, :], ACT.Relu, bias=gb1[:, c:c + 1]).then_inc(ghid_act, 1)

            def gra_step(at):
                if at(0):
                    root(gra, at(0), 4)
                    wait_past(act, gra.summed, at(0).n)
                    normalise(gra, at(0), 4, ACT.Relu)
                if at(1):
                    sums_out(gra, at(1), bank[6], mout)

            def out_step(at):
                t = at(0)
                act.wait_ge(n_out.turned, t.n + 1)
                S.activation(nT[:, t.slot(), :], bank[0][:, :], ACT.Copy).then_inc(n_out.turned_out, 1)

            def sumsT_out(w, t):
                act.wait_ge(w.summed, t.n + 1)
                S.activation(nT[:, t.slot(), :], bank[t.slot()][:, :], ACT.Copy).then_inc(w.sums_out, 1)

            def w_x2_step(at):
                if at(3):
                    sumsT_out(w_x2, at(3))
                if at(0):
                    root(wag, at(0), TILES)
                if at(5):
                    x2_roots(at(5))
                if at(1):
                    wait_past(act, xw_ready, at(1).n - 1)
                    normalise(wag, at(1), TILES, ACT.Relu, xn2(at(1)), rows4(at(1)))
                if at(6):
                    h2_out(w_x2, at(6))

            def w_gcn_step(at):
                if at(5):
                    hidden_half(at(5))
                if at(4):
                    act.wait_ge(n_gcn.turned, at(4).n + 1)
                    S.activation(nT[:, at(4).slot(), :], bank[0][:, :], ACT.Copy).then_inc(n_gcn.turned_out, 1)

            def w_x3_step(at):
                t = at(3)
                if t:
                    act.wait_ge(own_added, t.n + 1)
                    wait_past(act, n_x3.result, t.n - 1)
                    for k in range(4):
                        f = slice(128 * k, 128 * k + 128)
                        ins = S.activation(nT[:, t.slot(), f], ntmp[:, t.slot(), f], ACT.Copy, scale=dinv_x3[:, t.slot(4), k:k + 1])
                    ins.then_inc(gc2.out_ready, 1)

            def w_out_step(at):
                if at(3):
                    sumsT_out(w_out, at(3))
                if at(0):
                    root(gra, at(0), TILES)
                if at(1):
                    wait_past(act, gra.summed, at(1).n - 1)
                    for s in range(TILES):
                        if s == 0:
                            act.wait_ge(gra.norm_ready, at(1).n + 1)
                        for to in (high[:, at(1).slot(), s, :].bitcast(F32R), xn2(at(1))[:, s, :]):
                            ins = S.activation(to, rows4(at(1))[:, s, :], ACT.Relu, bias=nmr[:, at(1).slot(), s:s + 1],
                                               scale=rstd[:, at(1).slot(), s:s + 1])
                    ins.then_inc(gra.xn_ready, 1)

            def edges(step, lag):
                return Part(EDGE_TURNS, lag, step)

            def all_nodes(step, lag):
                return Part(NODE_TURNS, lag, step)

            passes(act, nothing, [
                (nothing, all_nodes(w_x2_step, 6)),
                (nothing, all_nodes(w_gcn_step, 5)),
                (nothing, all_nodes(w_x3_step, 3)),
                (nothing, all_nodes(w_out_step, 3)),
            ], [
                (nothing, edges(wag_step, 1), all_nodes(h2_step, 1)),
                (nothing, edges(plain_out(gc1), 0), all_nodes(gcn_step, 0)),
                (nothing, edges(plain_out(gc2), 0)),
                (nothing, edges(gra_step, 1), all_nodes(out_step, 0)),
            ])

        @block.tensor
        def _(pe):
            T = nc.tensor
            pe.wait_ge(ready, 12)
            pe.wait_ge(loads, 16 * n_const)
            T.transpose(bank[0][:, 0:128], l1w[:, :], ident[:, :]).then_inc(wT_psum, 1)
            pe.wait_ge(counted, 6)
            for h in range(2):
                for nxt in range(2):
                    lo = HALF * h + nxt
                    ins = T.matmul(bank[6][0:HALF, 2 * h + nxt:2 * h + nxt + 1], below[:, lo:lo + HALF], ones[0:112, 0:1],
                                   start=True, stop=True)
            ins.then_inc(counts_psum, 1)
            pe.wait_ge(lag_ready, 1)
            T.transpose(bank[7][0:1, 0:128], lag_col[:, :], ident[:, :]).then_inc(lag_psum, 1)
            pe.wait_ge(wT_out, 1)
            pe.wait_ge(window_lists_set, 2)
            n = 0
            for h, buf in enumerate((nb, no)):
                of = window_lists(buf)
                for l in range(3):
                    for s in range(TILES):
                        if n >= 4:
                            pe.wait_ge(win_out, n - 3)
                        T.transpose(bank[n % 4][:, 0:HALF], of[:, WINDOW * l + 128 * s:WINDOW * l + 128 * s + 128], ident[0:HALF, 0:HALF]).then_inc(win_psum, 1)
                        n += 1

            def turn_rows(to, of):
                for s in range(4):
                    ins = T.transpose(to[:, 128 * s:128 * s + 128], of(s), ident[:, :])
                return ins

            def batch_sums(to, of, slot):
                for s2 in range(4):
                    f = slice(128 * s2, 128 * s2 + 128)
                    for s in range(4):
                        ins = T.matmul(to[:, f], eq[:, slot, s, f], of(s), start=(s == 0), stop=(s == 3))
                return ins

            def split_sums(to, t, tiles):
                for q in range(4):
                    f = slice(128 * q, 128 * q + 128)
                    for s in range(tiles):
                        for part in (low, high):
                            ins = T.matmul(to[:, f], eq[:, t.slot(), s, f].bitcast(F32R), part[:, t.slot(), s, :].bitcast(F32R),
                                           start=(s == 0 and part is low), stop=(s == tiles - 1 and part is high))
                return ins

            def mlp_step(at):
                t1, t2, t4 = at(1), at(2), at(4)
                if t2:
                    pe.wait_ge(turned_out, 3 * t2.n + 3)
                    wait_past(pe, hid_out, 2 * t2.n)
                    for c in range(2):
                        f = slice(128 * c, 128 * c + 128)
                        T.matmul(bank[3 + c][:, :], w1s[:, f], hTs[:, :], start=True, stop=False)
                        T.matmul(bank[3 + c][:, :], w1d[:, f], hTd[:, :], start=False, stop=False)
                        T.matmul(bank[3 + c][:, :], w1e[:, f], eT[:, :], start=False, stop=True).then_inc(hid_psum, 1)
                if t1:
                    pe.wait_ge(ea_loaded[t1.slot()], 16 * (t1.use() + (2 if last_turn(t1) else 1)))
                    pe.wait_ge(mlp.xn_ready, t1.n + 1)
                    wait_past(pe, turned_out, 3 * t1.n)
                    turn_rows(bank[0], lambda s: xn[:, s, :]).then_inc(turned, 1)
                    turn_rows(bank[1], lambda s: xn[:, 4 + s, :]).then_inc(turned, 1)
                    for s in range(4):
                        ins = T.transpose(bank[2][0:64, 128 * s:128 * s + 128], eav[:, t1.slot(), s, :], ident[:, :])
                    ins.then_inc(turned, 1)
                if t4:
                    pe.wait_ge(msg_split, t4.n + 1)
                    pe.wait_ge(mlp.eq_ready, t4.n + 1)
                    wait_past(pe, mlp.out_ready, t4.n)
                    split_sums(bank[6], t4, 4).then_inc(mlp.summed, 1)
                if t2:
                    pe.wait_ge(hid_out, 2 * t2.n + 2)
                    wait_past(pe, msg_split, t2.n)
                    for s in range(4):
                        f = slice(128 * s, 128 * s + 128)
                        for c in range(2):
                            T.matmul(bank[5][:, f], ehid[:, c, f], w2c[:, c, :], start=(c == 0), stop=False)
                        ins = T.matmul(bank[5][:, f], ones[:, :].bitcast(F32R), bias_split[:, 2, :].bitcast(F32R), start=False, stop=True)
                    ins.then_inc(msg_psum, 1)

            run(pe, Part(EDGE_TURNS, 4, mlp_step))

            def wag_step(at):
                t = at(0)
                if t:
                    pe.wait_ge(xw_ready, t.n + 1)
                    pe.wait_ge(wag.eq_ready, t.n + 1)
                    wait_past(pe, aggT_out, t.n)
                    for s in range(4):
                        ins = T.matmul(bank[0][:, :], xw[:, 0, s, :], eq[:, t.slot(), s, :], start=(s == 0), stop=(s == 3))
                    ins.then_inc(aggT_psum, 1)
                    pe.wait_ge(aggT_out, t.n + 1)
                    wait_past(pe, wag.out_ready, t.n)
                    for s in range(4):
                        f = slice(128 * s, 128 * s + 128)
                        ins = T.matmul(bank[1][:, f], hTs[:, f], l1wT[:, :], start=True, stop=True)
                    ins.then_inc(wag.summed, 1)

            def plain_sums(e):
                def step(at):
                    t = at(0)
                    if t:
                        pe.wait_ge(e.gathered[t.slot()], 64 * (t.use() + 1))
                        pe.wait_ge(e.eq_ready, t.n + 1)
                        wait_past(pe, e.out_ready, t.n - 1)
                        batch_sums(bank[6 + t.slot()], lambda s: rows[:, t.slot(), s, :], t.slot()).then_inc(e.summed, 1)
                return step

            def gcn_step(at):
                new, old = at(0), at(1)
                if new:
                    pe.wait_ge(n_gcn.inputs_read, new.n + 1)
                    wait_past(pe, n_gcn.turned_out, new.n)
                    turn_rows(bank[0], lambda s: nt[:, new.slot(4), 128 * s:128 * s + 128]).then_inc(n_gcn.turned, 1)
                if old:
                    second_product(old)
                if new:
                    pe.wait_ge(n_gcn.turned_out, new.n + 1)
                    hidden(new, nT[:, 0, :])

            def second_product(t):
                pe.wait_ge(ghid_act, 2 * t.n + 2)
                pe.wait_ge(ghid_dve, 2 * t.n + 2)
                wait_past(pe, n_gcn.result, t.n)
                for s in range(4):
                    f = slice(128 * s, 128 * s + 128)
                    for c in range(4):
                        ins = T.matmul(bank[5][:, f], nhid[:, c, f], gw2[:, c, :], start=(c == 0), stop=(c == 3))
                ins.then_inc(n_gcn.product, 1)

            def hidden(t, of):
                for c in range(4):
                    T.matmul(bank[1 + c][:, :], gw1[:, 128 * c:128 * c + 128], of, start=True, stop=True).then_inc(ghid_psum, 1)

            def gra_step(at):
                t = at(0)
                if t:
                    pe.wait_ge(gra.xn_ready, t.n + 1)
                    pe.wait_ge(gra.eq_ready, t.n + 1)
                    wait_past(pe, gra.out_ready, t.n)
                    batch_sums(bank[6], lambda s: xn[:, s, :], t.slot()).then_inc(gra.summed, 1)

            def out_step(at):
                new, old = at(0), at(1)
                if new:
                    pe.wait_ge(node_loaded[new.slot(4)], n_out.loaded(new))
                    wait_past(pe, n_out.turned_out, new.n)
                    turn_rows(bank[0], lambda s: nb[:, new.slot(4), 128 * s:128 * s + 128]).then_inc(n_out.turned, 1)
                if old:
                    pe.wait_ge(n_out.turned_out, old.n + 1)
                    wait_past(pe, n_out.result, old.n)
                    for s in range(4):
                        f = slice(128 * s, 128 * s + 128)
                        ins = T.matmul(bank[1][:, f], nT[:, old.slot(), f], l3w[:, :], start=True, stop=True)
                    ins.then_inc(n_out.product, 1)

            def product_of(t, weight, bias, done):
                for s in range(4):
                    f = slice(128 * s, 128 * s + 128)
                    T.matmul(bank[2 + t.slot()][:, f], nT[:, t.slot(), f], weight[:, :], start=True, stop=False)
                    ins = T.matmul(bank[2 + t.slot()][:, f], ones[:, :].bitcast(F32R), bias_split[:, bias, :].bitcast(F32R), start=False, stop=True)
                ins.then_inc(done, 1)

            def sumsT(w, t, of):
                wait_past(pe, w.sums_out, t.n - 1)
                for s in range(TILES):
                    ins = T.matmul(bank[t.slot()][:, :], of[:, s, :], eq[:, t.slot(), s, :], start=(s == 0), stop=(s == TILES - 1))
                return ins

            def w_x2_step(at):
                t = at(2)
                if t:
                    pe.wait_ge(wag.eq_ready, t.n + 1)
                    pe.wait_ge(xw_ready, t.n + 1)
                    sumsT(w_x2, t, xw[:, t.slot(), :, :])
                    for q in range(4):
                        for s in range(TILES):
                            ins = T.matmul(bank[4 + t.slot(4)][:, 2 * q:2 * q + 2], eq[:, t.slot(), s, 128 * q:128 * q + 128].bitcast(F32R), ones[:, 0:2].bitcast(F32R),
                                           start=(s == 0), stop=(s == TILES - 1))
                    ins.then_inc(w_x2.summed, 1)
                if at(3):
                    pe.wait_ge(w_x2.sums_out, at(3).n + 1)
                    wait_past(pe, n_x2.inputs_read, at(3).n - 1)
                    product_of(at(3), l1wT, 0, product)

            def sums(to, t):
                for q in range(4):
                    f = slice(128 * q, 128 * q + 128)
                    for s in range(TILES):
                        ins = T.matmul(to[:, f], eq[:, t.slot(), s, f], rows4(t)[:, s, :], start=(s == 0), stop=(s == TILES - 1))
                return ins

            def w_gcn_step(at):
                if at(5):
                    t = at(5)
                    pe.wait_ge(n_gcn.turned_out, t.n + 1)
                    hidden(t, nT[:, t.slot(), :])
                if at(2):
                    t = at(2)
                    pe.wait_ge(gc1.eq_ready, t.n + 1)
                    pe.wait_ge(split_ready, t.n + 1)
                    wait_past(pe, n_gcn.inputs_read, t.n - 1)
                    split_sums(bank[6 + t.slot()], t, TILES).then_inc(gc1.summed, 1)
                if at(4):
                    t = at(4)
                    pe.wait_ge(n_gcn.inputs_read, t.n + 1)
                    wait_past(pe, n_gcn.turned_out, t.n)
                    turn_rows(bank[0], lambda s: nt[:, t.slot(4), 128 * s:128 * s + 128]).then_inc(n_gcn.turned, 1)
                if at(5):
                    second_product(at(5))

            def w_x3_step(at):
                if at(1):
                    t = at(1)
                    pe.wait_ge(gc2.eq_ready, t.n + 1)
                    pe.wait_ge(w_x3.gathered[t.slot(4)], 16 * TILES * (t.use(4) + 1))
                    wait_past(pe, own_added, t.n - 1)
                    sums(bank[6 + t.slot()], t).then_inc(gc2.summed, 1)

            def w_out_step(at):
                t = at(2)
                if t:
                    pe.wait_ge(out_split, t.n + 1)
                    wait_past(pe, w_out.sums_out, t.n - 1)
                    for s in range(TILES):
                        for part in (low, high):
                            ins = T.matmul(bank[t.slot()][:, :], part[:, t.slot(), s, :].bitcast(F32R), eq[:, t.slot(), s, :].bitcast(F32R),
                                           start=(s == 0 and part is low), stop=(s == TILES - 1 and part is high))
                    ins.then_inc(gra.summed, 1)
                if at(3):
                    pe.wait_ge(w_out.sums_out, at(3).n + 1)
                    wait_past(pe, n_out.result, at(3).n - 1)
                    product_of(at(3), l3w, 1, n_out.product)

            def edges(step, lag=0):
                return Part(EDGE_TURNS, lag, step)

            def all_nodes(step, lag):
                return Part(NODE_TURNS, lag, step)

            passes(pe, nothing, [
                (nothing, all_nodes(w_x2_step, 3)),
                (nothing, all_nodes(w_gcn_step, 5)),
                (nothing, all_nodes(w_x3_step, 1)),
                (nothing, all_nodes(w_out_step, 3)),
            ], [
                (nothing, edges(wag_step)),
                (nothing, edges(plain_sums(gc1)), all_nodes(gcn_step, 1)),
                (nothing, edges(plain_sums(gc2))),
                (nothing, edges(gra_step), all_nodes(out_step, 1)),
            ])


_INS = ["x", "src", "dst", "edge_attr_64", "edge_weight", "L0_gnn_W1", "L0_gnn_b1", "L0_gnn_W2", "L0_gnn_b2", "L1_gnn_W",
        "L1_gnn_b", "L2_gnn_W1", "L2_gnn_b1", "L2_gnn_W2", "L2_gnn_b2", "L3_gnn_W", "L3_gnn_b"]


def kernel(**inputs):
    import numpy as _np
    import concourse.bacc as _bacc
    from concourse import mybir as _mybir
    from concourse.bass_utils import run_bass_kernel_spmd as _run

    nc = _bacc.Bacc("TRN2", target_bir_lowering=False, num_devices=1)
    arrays, args = {}, []
    for name in _INS:
        a = _np.ascontiguousarray(inputs[name])
        arrays[f"in_{name}_dram"] = a
        args.append(nc.dram_tensor(f"in_{name}_dram", a.shape, _mybir.dt.from_np(a.dtype), kind="ExternalInput").ap())
    args.append(nc.dram_tensor("out_0_dram", (N, D), _mybir.dt.float32, kind="ExternalOutput").ap())
    build(nc, *args)
    r = _run(nc, [arrays], core_ids=[0])
    return r.results[0]["out_0_dram"]
```
